# Optimizing a Trainium2 kernel written in Bass

```python
import numpy as np
import jax
import jax.numpy as jnp

def _softmax(x, axis=-1):
    return jax.nn.softmax(x, axis=axis)

def _gelu(x):
    return jax.nn.gelu(x, approximate=True)

def _silu(x):
    return jax.nn.silu(x)

def _sigmoid(x):
    return jax.nn.sigmoid(x)

def _layernorm(x, axis=-1, eps=1e-05):
    m = jnp.mean(x, axis=axis, keepdims=True)
    v = jnp.var(x, axis=axis, keepdims=True)
    return (x - m) / jnp.sqrt(v + eps)

def _scatter_add(tgt, idx, src, axis=0):
    return tgt.at[idx].add(src)

def _segment_sum(src, seg, n):
    return jax.ops.segment_sum(src, seg, n)
kernel_name = 'mk_adaln_ffn_d1_seqx_r8_088538'

def setup_inputs(seed: int=0):
    np.random.seed(seed)
    _w = jnp.asarray

    def _rec_inputs():
        import jax
        import jax.numpy as jnp
        _rk = jax.random.key(seed)
        x = 7.22e-05 + 1 * jax.random.normal(jax.random.fold_in(_rk, 1), (32, 32, 128), jnp.float32)
        _lenS = 32 - jax.random.randint(jax.random.fold_in(_rk, 7), (32,), 0, max(1, 32 // 4) + 1, jnp.int32)
        _lenS2 = 32 - jax.random.randint(jax.random.fold_in(_rk, 8), (32,), 0, max(1, 32 // 4) + 1, jnp.int32)
        cond_64 = -0.104238 + 1.01173 * jax.random.normal(jax.random.fold_in(_rk, 11), (32, 64), jnp.float32)
        return (x, cond_64)
    x, cond_64 = _rec_inputs()

    def _L0_cond_setup():
        import jax, jax.numpy as jnp
        import numpy as np
        B, S, H = (4, 256, 128)
        E = 8
        M = 64
        K = 2
        N_SHARED = 2
        SM = M * N_SHARED
        G = 64
        GE_TEMP = 1.0
        ALPHA = 0.001
        SEQ_AUX = True
        NORM_TOPK = True
        COS_TEMP = 0.78
        CONS_ALPHA = 0.01
        LEAKY_SLOPE = 0.01
        EPS_COS = 1e-08

        def _leaky(x):
            return jnp.where(x >= 0, x, LEAKY_SLOPE * x)

        def _moe_forward(hidden_states, g, wt, wg, w_gate, w_up, w_down, sw_gate, sw_up, sw_down):
            b, s, h = hidden_states.shape
            x = hidden_states.reshape(-1, h)
            T = x.shape[0]
            logits_h = x @ wt.T
            logits_g = g @ wg.T
            logits_g = jnp.repeat(logits_g, s, axis=0)
            logits = (logits_h + logits_g / GE_TEMP) / (1.0 + 1.0 / GE_TEMP)
            scores = jax.nn.softmax(logits, axis=-1)
            topk_w, topk_idx = jax.lax.top_k(scores, K)
            if K > 1 and NORM_TOPK:
                topk_w = topk_w / (topk_w.sum(-1, keepdims=True) + 1e-20)
            onehot = jax.nn.one_hot(topk_idx.reshape(b, s * K), E, dtype=jnp.float32)
            ce = onehot.sum(1) / (s * K / E)
            aux_loss = (ce * scores.reshape(b, s, E).mean(1)).sum(1).mean() * ALPHA
            gp = _leaky(jnp.einsum('th,ehm->etm', x, w_gate))
            up = jnp.einsum('th,ehm->etm', x, w_up)
            y_all = jnp.einsum('etm,emh->eth', gp * up, w_down)
            y_sel = y_all[topk_idx, jnp.arange(T)[:, None], :]
            y = (y_sel * topk_w[..., None]).sum(1).reshape(b, s, h)
            p = _leaky(hidden_states @ sw_gate) * (hidden_states @ sw_up) @ sw_down
            y = y + p
            num = jnp.sum(y * p, -1)
            den = jnp.maximum(jnp.linalg.norm(y, axis=-1), EPS_COS) * jnp.maximum(jnp.linalg.norm(p, axis=-1), EPS_COS)
            closs = CONS_ALPHA * jnp.mean(num / den / (1.0 + COS_TEMP))
            return (y, aux_loss + closs)
        key = jax.random.key(seed)
        ks = jax.random.split(key, 12)
        sh = 1.0 / np.sqrt(H)
        sm = 1.0 / np.sqrt(M)
        ssm = 1.0 / np.sqrt(SM)
        sg = 1.0 / np.sqrt(G)
        return {'hidden_states': jax.random.normal(ks[0], (B, S, H), jnp.float32), 'g': jax.random.normal(ks[1], (B, G), jnp.float32), 'wt': jax.random.uniform(ks[2], (E, H), jnp.float32, -sh, sh), 'wg': jax.random.uniform(ks[3], (E, G), jnp.float32, -sg, sg), 'w_gate': jax.random.uniform(ks[4], (E, H, M), jnp.float32, -sh, sh), 'w_up': jax.random.uniform(ks[5], (E, H, M), jnp.float32, -sh, sh), 'w_down': jax.random.uniform(ks[6], (E, M, H), jnp.float32, -sm, sm), 'sw_gate': jax.random.uniform(ks[7], (H, SM), jnp.float32, -sh, sh), 'sw_up': jax.random.uniform(ks[8], (H, SM), jnp.float32, -sh, sh), 'sw_down': jax.random.uniform(ks[9], (SM, H), jnp.float32, -ssm, ssm)}
    _L0_cond_all = _L0_cond_setup()
    _L0_cond_in = {k: v for k, v in _L0_cond_all.items() if k in ('wt', 'wg', 'w_gate', 'w_up', 'w_down', 'sw_gate', 'sw_up', 'sw_down')}
    del _L0_cond_all

    def _L0_ffn_setup():
        import jax, jax.numpy as jnp
        import numpy as np
        S, B, H = (256, 1, 128)
        N_HEADS = 16
        HEAD_DIM = H // N_HEADS
        E, K, F = (8, 2, 256)
        EPS = 1e-05

        def layernorm(x, w, b):
            mu = jnp.mean(x, axis=-1, keepdims=True)
            var = jnp.mean(jnp.square(x - mu), axis=-1, keepdims=True)
            return (x - mu) * jax.lax.rsqrt(var + EPS) * w + b
        key = jax.random.key(seed)
        ks = jax.random.split(key, 8)
        std = 0.02
        return {'x': jax.random.normal(ks[0], (S, B, H), dtype=jnp.float32), 'ln1_w': jnp.ones((H,), jnp.float32), 'ln1_b': jnp.zeros((H,), jnp.float32), 'in_proj_w': jax.random.normal(ks[1], (3 * H, H), jnp.float32) * std, 'in_proj_b': jnp.zeros((3 * H,), jnp.float32), 'out_proj_w': jax.random.normal(ks[2], (H, H), jnp.float32) * std, 'out_proj_b': jnp.zeros((H,), jnp.float32), 'ln2_w': jnp.ones((H,), jnp.float32), 'ln2_b': jnp.zeros((H,), jnp.float32), 'router_w': jax.random.normal(ks[3], (E, H), jnp.float32) * std, 'w1': jax.random.normal(ks[4], (E, H, F), jnp.float32) * std, 'w2': jax.random.normal(ks[5], (E, F, H), jnp.float32) * std}
    _L0_ffn_all = _L0_ffn_setup()
    _L0_ffn_in = {k: v for k, v in _L0_ffn_all.items() if k in ('ln1_w', 'ln1_b', 'in_proj_w', 'in_proj_b', 'out_proj_w', 'out_proj_b', 'ln2_w', 'ln2_b', 'router_w', 'w1', 'w2')}
    del _L0_ffn_all
    return {'x': x, 'cond_64': cond_64, 'L0_cond_wt': _L0_cond_in['wt'], 'L0_cond_wg': _L0_cond_in['wg'], 'L0_cond_w_gate': _L0_cond_in['w_gate'], 'L0_cond_w_up': _L0_cond_in['w_up'], 'L0_cond_w_down': _L0_cond_in['w_down'], 'L0_cond_sw_gate': _L0_cond_in['sw_gate'], 'L0_cond_sw_up': _L0_cond_in['sw_up'], 'L0_cond_sw_down': _L0_cond_in['sw_down'], 'L0_ffn_ln1_w': _L0_ffn_in['ln1_w'], 'L0_ffn_ln1_b': _L0_ffn_in['ln1_b'], 'L0_ffn_in_proj_w': _L0_ffn_in['in_proj_w'], 'L0_ffn_in_proj_b': _L0_ffn_in['in_proj_b'], 'L0_ffn_out_proj_w': _L0_ffn_in['out_proj_w'], 'L0_ffn_out_proj_b': _L0_ffn_in['out_proj_b'], 'L0_ffn_ln2_w': _L0_ffn_in['ln2_w'], 'L0_ffn_ln2_b': _L0_ffn_in['ln2_b'], 'L0_ffn_router_w': _L0_ffn_in['router_w'], 'L0_ffn_w1': _L0_ffn_in['w1'], 'L0_ffn_w2': _L0_ffn_in['w2']}

def reference(x, cond_64, L0_cond_wt, L0_cond_wg, L0_cond_w_gate, L0_cond_w_up, L0_cond_w_down, L0_cond_sw_gate, L0_cond_sw_up, L0_cond_sw_down, L0_ffn_ln1_w, L0_ffn_ln1_b, L0_ffn_in_proj_w, L0_ffn_in_proj_b, L0_ffn_out_proj_w, L0_ffn_out_proj_b, L0_ffn_ln2_w, L0_ffn_ln2_b, L0_ffn_router_w, L0_ffn_w1, L0_ffn_w2):
    import jax
    import jax.numpy as jnp

    def _L0_cond_ref(hidden_states, g, wt, wg, w_gate, w_up, w_down, sw_gate, sw_up, sw_down):
        import jax, jax.numpy as jnp
        import numpy as np
        B, S, H = (4, 256, 128)
        E = 8
        M = 64
        K = 2
        N_SHARED = 2
        SM = M * N_SHARED
        G = 64
        GE_TEMP = 1.0
        ALPHA = 0.001
        SEQ_AUX = True
        NORM_TOPK = True
        COS_TEMP = 0.78
        CONS_ALPHA = 0.01
        LEAKY_SLOPE = 0.01
        EPS_COS = 1e-08

        def _leaky(x):
            return jnp.where(x >= 0, x, LEAKY_SLOPE * x)

        def _moe_forward(hidden_states, g, wt, wg, w_gate, w_up, w_down, sw_gate, sw_up, sw_down):
            b, s, h = hidden_states.shape
            x = hidden_states.reshape(-1, h)
            T = x.shape[0]
            logits_h = x @ wt.T
            logits_g = g @ wg.T
            logits_g = jnp.repeat(logits_g, s, axis=0)
            logits = (logits_h + logits_g / GE_TEMP) / (1.0 + 1.0 / GE_TEMP)
            scores = jax.nn.softmax(logits, axis=-1)
            topk_w, topk_idx = jax.lax.top_k(scores, K)
            if K > 1 and NORM_TOPK:
                topk_w = topk_w / (topk_w.sum(-1, keepdims=True) + 1e-20)
            onehot = jax.nn.one_hot(topk_idx.reshape(b, s * K), E, dtype=jnp.float32)
            ce = onehot.sum(1) / (s * K / E)
            aux_loss = (ce * scores.reshape(b, s, E).mean(1)).sum(1).mean() * ALPHA
            gp = _leaky(jnp.einsum('th,ehm->etm', x, w_gate))
            up = jnp.einsum('th,ehm->etm', x, w_up)
            y_all = jnp.einsum('etm,emh->eth', gp * up, w_down)
            y_sel = y_all[topk_idx, jnp.arange(T)[:, None], :]
            y = (y_sel * topk_w[..., None]).sum(1).reshape(b, s, h)
            p = _leaky(hidden_states @ sw_gate) * (hidden_states @ sw_up) @ sw_down
            y = y + p
            num = jnp.sum(y * p, -1)
            den = jnp.maximum(jnp.linalg.norm(y, axis=-1), EPS_COS) * jnp.maximum(jnp.linalg.norm(p, axis=-1), EPS_COS)
            closs = CONS_ALPHA * jnp.mean(num / den / (1.0 + COS_TEMP))
            return (y, aux_loss + closs)
        y, _ = _moe_forward(hidden_states, g, wt, wg, w_gate, w_up, w_down, sw_gate, sw_up, sw_down)
        return y

    def _L0_ffn_ref(x, ln1_w, ln1_b, in_proj_w, in_proj_b, out_proj_w, out_proj_b, ln2_w, ln2_b, router_w, w1, w2):
        import jax, jax.numpy as jnp
        import numpy as np
        S, B, H = (256, 1, 128)
        N_HEADS = 16
        HEAD_DIM = H // N_HEADS
        E, K, F = (8, 2, 256)
        EPS = 1e-05

        def layernorm(x, w, b):
            mu = jnp.mean(x, axis=-1, keepdims=True)
            var = jnp.mean(jnp.square(x - mu), axis=-1, keepdims=True)
            return (x - mu) * jax.lax.rsqrt(var + EPS) * w + b
        s, b, h = x.shape
        hn = layernorm(x, ln1_w, ln1_b)
        qkv = hn @ in_proj_w.T + in_proj_b
        q, k, v = jnp.split(qkv, 3, axis=-1)
        q = q.reshape(s, b, N_HEADS, HEAD_DIM)
        k = k.reshape(s, b, N_HEADS, HEAD_DIM)
        v = v.reshape(s, b, N_HEADS, HEAD_DIM)
        scores = jnp.einsum('sbnd,tbnd->bnst', q, k) / np.sqrt(HEAD_DIM)
        causal = jnp.tril(jnp.ones((s, s), bool))
        scores = jnp.where(causal[None, None], scores, -jnp.inf)
        probs = jax.nn.softmax(scores, axis=-1)
        attn = jnp.einsum('bnst,tbnd->sbnd', probs, v).reshape(s, b, h)
        attn = attn @ out_proj_w.T + out_proj_b
        x1 = x + attn
        hn2 = layernorm(x1, ln2_w, ln2_b).reshape(s * b, h)
        logits = hn2 @ router_w.T
        rp = jax.nn.softmax(logits, axis=-1)
        topw, topi = jax.lax.top_k(rp, K)
        gates = jnp.sum(jax.nn.one_hot(topi, E, dtype=hn2.dtype) * topw[..., None], axis=1)
        hmid = jax.nn.gelu(jnp.einsum('th,ehf->tef', hn2, w1), approximate=False)
        y = jnp.einsum('tef,efh->th', hmid * gates[:, :, None], w2)
        return x1 + y.reshape(s, b, h)
    x = x + _L0_ffn_ref(_L0_cond_ref(x, cond_64, L0_cond_wt, L0_cond_wg, L0_cond_w_gate, L0_cond_w_up, L0_cond_w_down, L0_cond_sw_gate, L0_cond_sw_up, L0_cond_sw_down), L0_ffn_ln1_w, L0_ffn_ln1_b, L0_ffn_in_proj_w, L0_ffn_in_proj_b, L0_ffn_out_proj_w, L0_ffn_out_proj_b, L0_ffn_ln2_w, L0_ffn_ln2_b, L0_ffn_router_w, L0_ffn_w1, L0_ffn_w2)
    return x

_drawn_inputs = setup_inputs


def setup_inputs(seed=0):
    import zlib

    import numpy as np

    out = dict(_drawn_inputs(seed))
    spreads = {'L0_ffn_ln1_w': (1.0, 0.6),
     'L0_ffn_ln1_b': (0.0, 0.8),
     'L0_ffn_in_proj_b': (0.0, 0.326),
     'L0_ffn_out_proj_b': (0.0, 0.1),
     'L0_ffn_ln2_w': (1.0, 0.6),
     'L0_ffn_ln2_b': (0.0, 0.8)}
    factors = {'L0_ffn_in_proj_w': 2.742,
     'L0_ffn_router_w': 7.191,
     'L0_ffn_w1': 6.174,
     'L0_ffn_w2': 6.081}
    for name, (base, spread) in spreads.items():
        noise = np.random.default_rng([zlib.crc32(name.encode()), seed]).standard_normal(out[name].shape)
        drawn = base * np.exp(spread * noise) if base else spread * noise
        out[name] = jnp.asarray(drawn.astype(out[name].dtype))
    for name, factor in factors.items():
        out[name] = (out[name] * factor).astype(out[name].dtype)
    return out
```

```python
from contextlib import ExitStack

import concourse.bass as bass
from concourse import mybir

F32 = mybir.dt.float32
F32R = mybir.dt.float32r
I32 = mybir.dt.int32
ALU = mybir.AluOpType
ACT = mybir.ActivationFunctionType
AX_X = mybir.AxisListType.X

P = 128
HALVES = 2
BATCH = 32
SEQ = 32
D = 128
GROUPS = 4
GB = 4
N = GROUPS * P
NB = GROUPS * GB
E = 8
M = 64
CB = E * M // P + 1
ROUTED = CB - 1
SHARED = CB - 1
F = 256
FB = E * F // P
HEADS = 16
HD = D // HEADS
HG = 4
RT = HEADS // HG
EPS = 1e-5
LEAK = 0.01
MASKED = -1e30
RSQRT_SEED = 0x5F3759DF

ROW_BQ, ROW_BK, ROW_BV, ROW_LN1W, ROW_LN1B, ROW_LN2W, ROW_LN2B = range(7)
ROW_WT, ROW_ROUTER, ROWS = 7, 15, 23
GROW_WG, GROWS = 32, 40


def build(nc, x, cond, wt, wg, w_gate, w_up, w_down, sw_gate, sw_up, sw_down, ln1_w, ln1_b, in_w, in_b,
          out_w, out_b, ln2_w, ln2_b, router_w, w1, w2, out):
    with ExitStack() as ctx:
        def sb(name, shape, dt=F32):
            return ctx.enter_context(nc.sbuf_tensor(name, shape, dt))

        def bank(name):
            return ctx.enter_context(nc.psum_tensor(name, [P, N], F32))

        def sem(name):
            return ctx.enter_context(nc.semaphore(name))

        b_h0 = bank("b_h0")
        b_h1 = bank("b_h1")
        b_w = bank("b_w")
        b_y = bank("b_y")
        b_s0 = bank("b_s0")
        b_s1 = bank("b_s1")
        b_t = bank("b_t")
        b_o = bank("b_o")
        b_s = [b_s0, b_s1]
        b_h = [b_h0, b_h1]

        x_tok = sb("x_tok", [P, HALVES, GROUPS, D])
        rows = sb("rows", [ROWS, D])
        grows = sb("grows", [GROWS, M])
        cols = sb("cols", [P, ROWS])
        gcols = sb("gcols", [M, GROWS])
        cond4 = sb("cond4", [M, GB, SEQ])
        wgate = sb("wgate", [P, CB, P])
        wup = sb("wup", [P, CB, P])
        wdown = sb("wdown", [P, CB, D])
        wgate_h, wgate_l = sb("wgate_h", [P, CB, P], F32R), sb("wgate_l", [P, CB, P], F32R)
        wup_h, wup_l = sb("wup_h", [P, CB, P], F32R), sb("wup_l", [P, CB, P], F32R)
        proj = sb("proj", [P, 4, D])
        projT = sb("projT", [P, 4, D])
        qkT_h, qkT_l = sb("qkT_h", [P, 2, D], F32R), sb("qkT_l", [P, 2, D], F32R)
        bo = sb("bo", [P, D])
        w1_s = sb("w1_s", [P, FB, P])
        w2_s = sb("w2_s", [P, FB, D])
        w1_h, w1_l = sb("w1_h", [P, FB, P], F32R), sb("w1_l", [P, FB, P], F32R)
        w2_h, w2_l = sb("w2_h", [P, FB, D], F32R), sb("w2_l", [P, FB, D], F32R)

        ident = sb("ident", [P, P])
        ident_r = sb("ident_r", [SEQ, GB, SEQ], F32R)
        causal = sb("causal", [SEQ, SEQ])
        causal_r = sb("causal_r", [SEQ, SEQ], F32R)
        head16 = sb("head16", [P, RT, HG])
        headmask = sb("headmask", [P, HG])
        vmask = sb("vmask", [P, HG, HD])
        sel_r = sb("sel_r", [2 * E, E, P], F32R)
        selp_r = sb("selp_r", [2 * E, ROUTED, P], F32R)
        prio = sb("prio", [P, E])

        xT = sb("xT", [P, HALVES, N])
        xT_h, xT_l = sb("xT_h", [P, HALVES, N], F32R), sb("xT_l", [P, HALVES, N], F32R)
        gate_s = sb("gate_s", [P, 2, N])
        leaky = sb("leaky", [P, 2, N])
        gu = sb("gu", [P, 2, N])
        wb_s = sb("wb_s", [P, 2, N])
        mid = sb("mid", [P, 2, N])
        y_tok = sb("y_tok", [P, HALVES, GROUPS, D])
        hn = sb("hn", [P, 2, GROUPS, D])
        hT = sb("hT", [P, 2, N])
        hT_h, hT_l = sb("hT_h", [P, 2, N], F32R), sb("hT_l", [P, 2, N], F32R)
        h2_h, h2_l = sb("h2_h", [P, HALVES, N], F32R), sb("h2_l", [P, HALVES, N], F32R)
        qT = sb("qT", [P, N])
        kT = sb("kT", [P, N])
        kx = sb("kx", [P, HG, N])
        vc = sb("vc", [P, NB, RT, HD])
        vx = sb("vx", [P, NB, RT, HG, HD])
        mx = sb("mx", [P, RT, GROUPS * HG])
        prob = sb("prob", [P, RT, N])
        sel = prob[0:2 * E, 0:2].rearrange("k r (e p) -> k (r e) p", p=P)
        probT = sb("probT", [P, RT, N])
        rsum = sb("rsum", [P, GROUPS * HEADS])
        att = sb("att", [P, GROUPS, D])
        attT = sb("attT", [P, N])
        x1_tok = sb("x1_tok", [P, HALVES, GROUPS, D])
        p_h, p_l = sb("p_h", [P, 2, N], F32R), sb("p_l", [P, 2, N], F32R)
        gel = w1_s[:, 0:FB // 2].rearrange("p (s b) q -> p s (b q)", s=2)
        pm = w1_s[:, FB // 2:FB].rearrange("p (s b) q -> p s (b q)", s=2)
        yT = w2_s[:, 0:GROUPS].rearrange("p b q -> p (b q)")
        o_tok = w2_s[:, GROUPS:3 * GROUPS].rearrange("p (c g) h -> p c g h", c=HALVES)
        stat6 = sb("stat6", [P, GROUPS, 6])
        stat2 = sb("stat2", [P, GROUPS, 2])
        lnw = sb("lnw", [P, 3, GROUPS])
        rt = sb("rt", [P, 8, GROUPS, E])
        rs = sb("rs", [P, 8, GROUPS])
        expo = sb("expo", [P, GROUPS, E])
        wsplit = sb("wsplit", [P, GROUPS, 2 * E], F32R)
        gT = sb("gT", [2 * E, 2, N], F32R)

        ld_x = [sem("ld_x0"), sem("ld_x1")]
        ld_rows, ld_cond, ld_shared, ld_gate, ld_up, ld_down, ld_proj, ld_w1, ld_w2 = (
            sem(s) for s in ("ld_rows", "ld_cond", "ld_shared", "ld_gate", "ld_up", "ld_down", "ld_proj",
                             "ld_w1", "ld_w2"))
        pool_const, pool_chain, pool_mid, pool_yb, pool_vx, pool_xo, pool_lo, pool_w1, pool_w2 = (
            sem(s) for s in ("pool_const", "pool_chain", "pool_mid", "pool_yb", "pool_vx", "pool_xo",
                             "pool_lo", "pool_w1", "pool_w2"))
        act_cols, act_x, act_proj, act_g, act_wb, act_gT, act_y, act_hT, act_qkv, act_exp, act_pT = (
            sem(s) for s in ("act_cols", "act_x", "act_proj", "act_g", "act_wb", "act_gT", "act_y", "act_hT",
                             "act_qkv", "act_exp", "act_pT"))
        act_aT, act_re, act_gel, act_yT, act_w1, act_w2, act_wh = (
            sem(s) for s in ("act_aT", "act_re", "act_gel", "act_yT", "act_w1", "act_w2", "act_wh"))
        dve_chain, dve_const, dve_xh, dve_x, dve_w, dve_gu, dve_split, dve_ld, dve_hn = (
            sem(s) for s in ("dve_chain", "dve_const", "dve_xh", "dve_x", "dve_w", "dve_gu", "dve_split",
                             "dve_ld", "dve_hn"))
        dve_hh, dve_hl, dve_kx, dve_dif, dve_att, dve_x1, dve_pm, dve_ph, dve_out, dve_qk = (
            sem(s) for s in ("dve_hh", "dve_hl", "dve_kx", "dve_dif", "dve_att", "dve_x1", "dve_pm", "dve_ph",
                             "dve_out", "dve_qk"))
        pe_x, pe_cols, pe_proj, pe_g, pe_u, pe_wb, pe_down, pe_log, pe_gT, pe_hT = (
            sem(s) for s in ("pe_x", "pe_cols", "pe_proj", "pe_g", "pe_u", "pe_wb", "pe_down", "pe_log",
                             "pe_gT", "pe_hT"))
        pe_q, pe_k, pe_v, pe_s, pe_pT, pe_pv, pe_sum, pe_aT, pe_o, pe_h, pe_y, pe_yT = (
            sem(s) for s in ("pe_q", "pe_k", "pe_v", "pe_s", "pe_pT", "pe_pv", "pe_sum", "pe_aT", "pe_o",
                             "pe_h", "pe_y", "pe_yT"))
        st_out = sem("st_out")

        ORDER = [SHARED, 0, 1, 2, 3]
        block = ctx.enter_context(nc.Block())

        def tile_rows(ap, c, b):
            return ap.rearrange("s (c g b) h -> c b s g h", c=HALVES, g=GROUPS)[c, b]

        @block.sync
        def _(sp):
            for b in range(GB):
                sp.dma_start(x_tok[b * SEQ:(b + 1) * SEQ, 0], tile_rows(x, 0, b)).then_inc(ld_x[0], 16)
            sp.dma_start(wgate[:, SHARED, :], sw_gate).then_inc(ld_shared, 16)
            sp.dma_start(wup[:, SHARED, :], sw_up).then_inc(ld_shared, 16)
            sp.dma_start(wgate[:, 0:SHARED, :].rearrange("h j (u m) -> h (j u) m", m=M),
                         w_gate.rearrange("e h m -> h e m")).then_inc(ld_gate, 16)
            sp.dma_start(wup[:, 0:SHARED, :].rearrange("h j (u m) -> h (j u) m", m=M),
                         w_up.rearrange("e h m -> h e m")).then_inc(ld_up, 16)
            sp.dma_start(wdown[:, 0:SHARED, :],
                         w_down.rearrange("e m h -> (e m) h").rearrange("(j p) h -> p j h", p=P)).then_inc(ld_down, 16)
            sp.dma_start(wdown[:, SHARED, :], sw_down).then_inc(ld_down, 16)
            for b in range(GB):
                sp.dma_start(x_tok[b * SEQ:(b + 1) * SEQ, 1], tile_rows(x, 1, b)).then_inc(ld_x[1], 16)
            sp.dma_start(proj[:, 0:3, :], in_w.rearrange("(k p) h -> p k h", p=P)).then_inc(ld_proj, 16)
            sp.dma_start(proj[:, 3, :], out_w).then_inc(ld_proj, 16)
            sp.dma_start(bo[:], out_b.partition_broadcast(P)).then_inc(ld_proj, 16)
            sp.dma_start(w1_s[:].rearrange("h (e b) p -> h e (b p)", e=E),
                         w1.rearrange("e h f -> h e f")).then_inc(ld_w1, 16)
            sp.dma_start(w2_s[:], w2.rearrange("e (b p) h -> p (e b) h", p=P)).then_inc(ld_w2, 16)
            for c in range(HALVES):
                sp.wait_ge(dve_out, c + 1)
                for b in range(GB):
                    sp.dma_start(tile_rows(out, c, b), o_tok[b * SEQ:(b + 1) * SEQ, c]).then_inc(st_out, 16)
            sp.wait_ge(st_out, 16 * GB * HALVES)

        @block.gpsimd
        def _(pool):
            chain = [0]

            def link(ins):
                chain[0] += 1
                ins.then_inc(pool_chain, 1)
                pool.wait_ge(pool_chain, chain[0])

            link(pool.memset(ident[:], 0.0))
            pool.affine_select(out=ident[:], in_=ident[:], compare_op=ALU.not_equal, fill=1.0, base=0,
                               pattern=[[-1, P]], channel_multiplier=1).then_inc(pool_const, 1)
            link(pool.memset(sel, 0.0))
            for part in range(2):
                link(pool.affine_select(out=sel, in_=sel, compare_op=ALU.not_equal, fill=1.0, base=-E * part,
                                        pattern=[[-1, E], [0, P]], channel_multiplier=1))
            link(pool.memset(causal[:], 0.0))
            link(pool.affine_select(out=causal[:], in_=causal[:], compare_op=ALU.is_ge, fill=MASKED, base=0,
                                    pattern=[[-1, SEQ]], channel_multiplier=1))
            link(pool.memset(head16[:], 1.0))
            link(pool.affine_select(out=head16[:], in_=head16[:], compare_op=ALU.is_ge, fill=0.0, base=0,
                                    pattern=[[-SEQ, RT], [-HD, HG]], channel_multiplier=1))
            link(pool.affine_select(out=head16[:], in_=head16[:], compare_op=ALU.is_ge, fill=0.0, base=HD - 1,
                                    pattern=[[SEQ, RT], [HD, HG]], channel_multiplier=-1))
            link(pool.memset(vmask[:], 1.0))
            link(pool.affine_select(out=vmask[:], in_=vmask[:], compare_op=ALU.is_ge, fill=0.0, base=0,
                                    pattern=[[-SEQ, HG], [0, HD]], channel_multiplier=1))
            pool.affine_select(out=vmask[:], in_=vmask[:], compare_op=ALU.is_ge, fill=0.0, base=SEQ - 1,
                               pattern=[[SEQ, HG], [0, HD]], channel_multiplier=-1).then_inc(pool_const, 1)

            def mids(c, n):
                k, s = ROUTED * c + n, n % 2
                pool.wait_ge(dve_gu, CB * c + n + 2)
                pool.wait_ge(act_wb, k + 1)
                if k >= 2:
                    pool.wait_ge(pe_down, CB * (c if n >= 2 else c - 1) + (n if n >= 2 else n + 4))
                pool.tensor_tensor(mid[:, s], gu[:, (n + 1) % 2], wb_s[:, s], ALU.mult).then_inc(pool_mid, 1)

            def residual_bias(c):
                pool.wait_ge(act_y, c + 1)
                if c == 0:
                    pool.wait_ge(ld_proj, 48)
                pool.wait_ge(dve_hn, 2 * c + 1)
                pool.tensor_tensor(y_tok[:, c], y_tok[:, c], bo[:].unsqueeze(1).broadcast_to([P, GROUPS, D]),
                                   ALU.add).then_inc(pool_yb, 1)

            def spread_values(c):
                pool.wait_ge(act_qkv, 3 * c + 3)
                if c:
                    pool.wait_ge(pe_pv, RT * c)
                v = vc[:].rearrange("p b r d -> p (b r) d").unsqueeze(2).broadcast_to([P, NB * RT, HG, HD])
                pool.tensor_tensor(vx[:].rearrange("p b r h d -> p (b r) h d"), v,
                                   vmask[:].unsqueeze(1).broadcast_to([P, NB * RT, HG, HD]),
                                   ALU.mult).then_inc(pool_vx, 1)

            def residual_in(c):
                pool.wait_ge(dve_x1, c + 1)
                pool.tensor_tensor(x_tok[:, c], x_tok[:, c], x1_tok[:, c], ALU.add).then_inc(pool_xo, 1)

            def ffn_low(c, i):
                k = FB * c + i
                pool.wait_ge(dve_ph, k + 1)
                if k >= 2:
                    pool.wait_ge(pe_y, k - 1)
                pool.tensor_tensor(p_l[:, k % 2], pm[:, k % 2], p_h[:, k % 2].bitcast(F32),
                                   ALU.subtract).then_inc(pool_lo, 1)

            def weight_low(which, i):
                full, high, low, src, dst = ((w1_s, w1_h, w1_l, act_w1, pool_w1), (w2_s, w2_h, w2_l, act_w2, pool_w2))[which]
                pool.wait_ge(src, i + 1)
                b = slice(4 * i, 4 * i + 4)
                pool.tensor_tensor(low[:, b], full[:, b], high[:, b].bitcast(F32), ALU.subtract).then_inc(dst, 1)

            for n in range(ROUTED):
                mids(0, n)
            residual_bias(0)
            for n in range(ROUTED):
                mids(1, n)
                if n == 0:
                    spread_values(0)
            residual_bias(1)
            for i in range(FB // 4):
                weight_low(0, i)
            for i in range(FB // 4):
                weight_low(1, i)
            residual_in(0)
            for i in range(FB):
                ffn_low(0, i)
                if i == 4:
                    spread_values(1)
            residual_in(1)
            for i in range(FB):
                ffn_low(1, i)

        @block.scalar
        def _(act):
            for at, src in ((ROW_BQ, in_b.rearrange("(k h) -> k h", k=3)), (ROW_LN1W, ln1_w.unsqueeze(0)),
                            (ROW_LN1B, ln1_b.unsqueeze(0)), (ROW_LN2W, ln2_w.unsqueeze(0)),
                            (ROW_LN2B, ln2_b.unsqueeze(0)), (ROW_WT, wt), (ROW_ROUTER, router_w)):
                act.dma_start(rows[at:at + src.shape[0], :], src).then_inc(ld_rows, 16)
            act.dma_start(grows[0:GROW_WG, :], cond).then_inc(ld_cond, 16)
            act.dma_start(grows[GROW_WG:GROWS, :], wg).then_inc(ld_cond, 16)

            def x_in(c):
                act.wait_ge(pe_x, c + 1)
                nc.scalar.copy(xT[:, c], b_s[c][:]).then_inc(act_x, 1)

            def gate_copy(c, n):
                k = CB * c + n
                act.wait_ge(pe_g, k + 1)
                if k >= 2:
                    act.wait_ge(dve_gu, k - 1)
                nc.scalar.copy(gate_s[:, k % 2], b_h0[:]).then_inc(act_g, 1)

            def weights_copy(c, n):
                k = ROUTED * c + n
                act.wait_ge(pe_wb, k + 1)
                if k >= 2:
                    act.wait_ge(pool_mid, k - 1)
                nc.scalar.copy(wb_s[:, n % 2], b_w[:]).then_inc(act_wb, 1)

            def route_exp(j, scale):
                act.wait_ge(dve_ld, j + 1)
                nc.scalar.activation(expo[:], rt[:, 0], ACT.Exp, scale=scale).then_inc(act_re, 1)

            def route_T(j):
                act.wait_ge(pe_gT, j + 1)
                nc.scalar.copy(gT[:, j // HALVES], b_w[0:2 * E, :]).then_inc(act_gT, 1)

            def y_copy(c):
                act.wait_ge(pe_down, CB * (c + 1))
                nc.scalar.copy(y_tok[:, c].rearrange("p g h -> p (g h)"), b_y[:]).then_inc(act_y, 1)

            def norm_T(j, slot, w, b):
                act.wait_ge(pe_hT, j + 1)
                if j >= 2:
                    act.wait_ge(dve_hl, j - 1)
                    act.wait_ge((pe_v, pe_log)[slot], 1 if slot == 0 else 3)
                nc.scalar.activation(hT[:, slot], b_t[:], ACT.Identity, scale=cols[:, w:w + 1],
                                     bias=cols[:, b:b + 1]).then_inc(act_hT, 1)

            def qkv_copy(c):
                act.wait_ge(pe_q, c + 1)
                if c:
                    act.wait_ge(pe_s, RT * c)
                nc.scalar.activation(qT[:], b_s0[:], ACT.Identity, scale=1.0,
                                     bias=cols[:, ROW_BQ:ROW_BQ + 1]).then_inc(act_qkv, 1)
                act.wait_ge(pe_k, c + 1)
                nc.scalar.activation(kT[:], b_s1[:], ACT.Identity, scale=1.0,
                                     bias=cols[:, ROW_BK:ROW_BK + 1]).then_inc(act_qkv, 1)
                act.wait_ge(pe_v, c + 1)
                if c:
                    act.wait_ge(pool_vx, c)
                nc.scalar.copy(vc[:].rearrange("p b r d -> p (b r d)"), b_t[:]).then_inc(act_qkv, 1)

            def soft_exp(c, r):
                act.wait_ge(dve_dif, RT * c + r + 1)
                nc.scalar.activation(prob[:, r], prob[:, r], ACT.Exp, scale=HD ** -0.5).then_inc(act_exp, 1)

            def prob_T(c, r):
                act.wait_ge(pe_pT, RT * c + r + 1)
                if c:
                    act.wait_ge(pe_sum, c)
                nc.scalar.copy(probT[:, r], b_t[:]).then_inc(act_pT, 1)

            def att_T(c):
                act.wait_ge(pe_aT, c + 1)
                if c:
                    act.wait_ge(pe_o, c)
                nc.scalar.activation(attT[:], b_s0[:], ACT.Identity, scale=1.0,
                                     bias=cols[:, ROW_BV:ROW_BV + 1]).then_inc(act_aT, 1)

            def gelu(c, i):
                k = FB * c + i
                act.wait_ge(pe_h, k + 1)
                if k == 0:
                    act.wait_ge(pool_w1, FB // 4)
                if k >= 2:
                    act.wait_ge(dve_pm, k - 1)
                nc.scalar.activation(gel[:, k % 2], b_h[i % 2][:], ACT.Gelu).then_inc(act_gel, 1)

            def y_out(c):
                act.wait_ge(pe_y, FB * (c + 1))
                if c:
                    act.wait_ge(pe_yT, c)
                nc.scalar.copy(yT[:], b_y[:]).then_inc(act_yT, 1)

            act.wait_ge(ld_shared, 32)
            for high, full in ((wgate_h, wgate), (wup_h, wup)):
                nc.scalar.copy(high[:, SHARED], full[:, SHARED]).then_inc(act_wh, 1)
            x_in(0)
            for high, full, ld in ((wgate_h, wgate, ld_gate), (wup_h, wup, ld_up)):
                act.wait_ge(ld, 16)
                nc.scalar.copy(high[:, 0:SHARED], full[:, 0:SHARED]).then_inc(act_wh, 1)
            act.wait_ge(pe_cols, 1)
            nc.scalar.copy(cols[:], b_t[:, 0:ROWS]).then_inc(act_cols, 1)
            nc.scalar.copy(gcols[:], b_t[0:M, ROWS:ROWS + GROWS]).then_inc(act_cols, 1)
            nc.scalar.copy(cond4[:], b_t[0:M, ROWS:ROWS + GROW_WG].unsqueeze(1).broadcast_to([M, GB, SEQ])
                           ).then_inc(act_cols, 1)
            gate_copy(0, 0)
            route_exp(0, 0.5)
            gate_copy(0, 1)
            route_T(0)
            for n in range(ROUTED):
                weights_copy(0, n)
                if n + 2 < CB:
                    gate_copy(0, n + 2)
                if n == 0:
                    x_in(1)
                if n == 1:
                    act.wait_ge(pe_proj, 1)
                    nc.scalar.copy(projT[:].rearrange("p k h -> p (k h)"), b_o[:]).then_inc(act_proj, 1)
            y_copy(0)
            gate_copy(1, 0)
            route_exp(1, 0.5)
            norm_T(0, 0, ROW_LN1W, ROW_LN1B)
            gate_copy(1, 1)
            route_T(1)
            weights_copy(1, 0)
            gate_copy(1, 2)
            qkv_copy(0)
            for r in range(RT):
                soft_exp(0, r)
                prob_T(0, r)
                if r < 3:
                    weights_copy(1, r + 1)
                if r < 2:
                    gate_copy(1, r + 3)
            y_copy(1)
            for i in range(FB // 4):
                act.wait_ge(ld_w1, 16)
                nc.scalar.copy(w1_h[:, 4 * i:4 * i + 4], w1_s[:, 4 * i:4 * i + 4]).then_inc(act_w1, 1)
            att_T(0)
            for i in range(FB // 4):
                act.wait_ge(ld_w2, 16)
                nc.scalar.copy(w2_h[:, 4 * i:4 * i + 4], w2_s[:, 4 * i:4 * i + 4]).then_inc(act_w2, 1)
            norm_T(1, 1, ROW_LN2W, ROW_LN2B)
            route_exp(2, 1.0)
            route_T(2)
            norm_T(2, 0, ROW_LN1W, ROW_LN1B)
            qkv_copy(1)
            for i in range(FB):
                gelu(0, i)
                if i == 4:
                    for r in range(RT):
                        soft_exp(1, r)
                if 5 <= i < 9:
                    prob_T(1, i - 5)
                if i == 10:
                    att_T(1)
                if i == 12:
                    norm_T(3, 1, ROW_LN2W, ROW_LN2B)
            route_exp(3, 1.0)
            route_T(3)
            y_out(0)
            for i in range(FB):
                gelu(1, i)
            y_out(1)

        @block.vector
        def _(dve):
            chain = [0]

            def link(ins):
                chain[0] += 1
                ins.then_inc(dve_chain, 1)
                dve.wait_ge(dve_chain, chain[0])

            def x_split(c):
                dve.wait_ge(act_x, c + 1)
                dve.tensor_copy(xT_h[:, c], xT[:, c]).then_inc(dve_xh, 1)
                dve.wait_ge(dve_xh, c + 1)
                dve.tensor_tensor(xT_l[:, c], xT[:, c], xT_h[:, c].bitcast(F32), ALU.subtract).then_inc(dve_x, 1)

            def w_low(i):
                full, high, low, b = ((wgate, wgate_h, wgate_l, slice(SHARED, CB)), (wup, wup_h, wup_l, slice(SHARED, CB)),
                                      (wgate, wgate_h, wgate_l, slice(0, SHARED)), (wup, wup_h, wup_l, slice(0, SHARED)))[i]
                dve.wait_ge(act_wh, i + 1)
                dve.tensor_tensor(low[:, b], full[:, b], high[:, b].bitcast(F32), ALU.subtract).then_inc(dve_w, 1)

            def route(j):
                if j >= 1:
                    dve.wait_ge(act_re, j)
                dve.wait_ge(pe_log, j + 1)
                L = b_w[:, 0:GROUPS * E].rearrange("p (g e) -> p g e", e=E)

                def wide(v):
                    return v.unsqueeze(2).broadcast_to([P, GROUPS, E])

                link(dve.tensor_reduce(rs[:, 0], L, AX_X, ALU.max))
                dve.tensor_tensor(rt[:, 0], L, wide(rs[:, 0]), ALU.subtract).then_inc(dve_ld, 1)
                dve.wait_ge(act_re, j + 1)
                link(dve.tensor_reduce(rs[:, 1], expo[:], AX_X, ALU.add))
                link(dve.reciprocal(rs[:, 2], rs[:, 1]))
                link(dve.tensor_tensor(rt[:, 1], expo[:], wide(rs[:, 2]), ALU.mult))
                pr = prio[:].unsqueeze(1).broadcast_to([P, GROUPS, E])
                for top in range(2):
                    s = rt[:, 1] if top == 0 else rt[:, 4]
                    link(dve.tensor_reduce(rs[:, 3], s, AX_X, ALU.max))
                    link(dve.tensor_tensor(rt[:, 2], s, wide(rs[:, 3]), ALU.is_equal))
                    link(dve.tensor_tensor(rt[:, 2], rt[:, 2], pr, ALU.mult))
                    link(dve.tensor_reduce(rs[:, 4], rt[:, 2], AX_X, ALU.max))
                    link(dve.tensor_tensor(rt[:, 3] if top == 0 else rt[:, 5], rt[:, 2], wide(rs[:, 4]), ALU.is_equal))
                    if top == 0:
                        link(dve.scalar_tensor_tensor(rt[:, 4], rt[:, 3], -4.0, rt[:, 1], ALU.mult, ALU.add))
                link(dve.tensor_tensor(rt[:, 6], rt[:, 3], rt[:, 5], ALU.add))
                link(dve.tensor_tensor(rt[:, 7], rt[:, 6], rt[:, 1], ALU.mult))
                if j < HALVES:
                    link(dve.tensor_reduce(rs[:, 5], rt[:, 7], AX_X, ALU.add))
                    link(dve.tensor_scalar(rs[:, 6], rs[:, 5], 1e-20, None, ALU.add))
                    link(dve.reciprocal(rs[:, 7], rs[:, 6]))
                    link(dve.tensor_tensor(rt[:, 7], rt[:, 7], wide(rs[:, 7]), ALU.mult))
                if j >= 1:
                    dve.wait_ge(pe_gT, j)
                link(dve.tensor_copy(wsplit[:, :, 0:E], rt[:, 7]))
                dve.tensor_tensor(wsplit[:, :, E:2 * E], rt[:, 7], wsplit[:, :, 0:E].bitcast(F32),
                                  ALU.subtract).then_inc(dve_split, 1)

            def gate_up(c, n):
                k = CB * c + n
                dve.wait_ge(act_g, k + 1)
                g = gate_s[:, k % 2]
                link(dve.scalar_tensor_tensor(leaky[:, k % 2], g, LEAK, g, ALU.mult, ALU.max))
                dve.wait_ge(pe_u, k + 1)
                if c and n < 2:
                    dve.wait_ge(pool_mid, ROUTED * c)
                    dve.wait_ge(pe_down, CB * c)
                elif n == 2:
                    dve.wait_ge(pe_down, CB * c + 1)
                elif n > 2:
                    dve.wait_ge(pool_mid, ROUTED * c + n - 2)
                dve.tensor_tensor(gu[:, n % 2], leaky[:, k % 2], b_h1[:], ALU.mult).then_inc(dve_gu, 1)

            def norm(j, slot, src):
                for g in range(GROUPS):
                    ins = dve.bn_stats(stat6[:, g], src[:, g])
                link(ins)
                for g in range(GROUPS):
                    ins = dve.bn_aggr(stat2[:, g], stat6[:, g])
                link(ins)
                v, y, t = (lnw[:, i] for i in range(3))
                link(dve.tensor_scalar(v, stat2[:, :, 1], EPS, None, ALU.add))
                link(dve.tensor_scalar(t.bitcast(I32), v.bitcast(I32), 1, None, ALU.arith_shift_right))
                link(dve.tensor_scalar(y.bitcast(I32), t.bitcast(I32), -1.0, float(RSQRT_SEED), ALU.mult, ALU.add))
                for _step in range(3):
                    link(dve.tensor_tensor(t, y, y, ALU.mult))
                    link(dve.scalar_tensor_tensor(t, t, -0.5, v, ALU.mult, ALU.mult))
                    link(dve.scalar_tensor_tensor(y, t, 1.5, y, ALU.add, ALU.mult))
                if j >= 2:
                    dve.wait_ge(pe_hT, j - 1)
                for g in range(GROUPS):
                    ins = dve.tensor_scalar(hn[:, slot, g], src[:, g], stat2[:, g, 0:1], y[:, g:g + 1],
                                            ALU.subtract, ALU.mult)
                ins.then_inc(dve_hn, 1)
                dve.wait_ge(dve_hn, j + 1)

            def norm_split(j, slot, high, low):
                dve.wait_ge(act_hT, j + 1)
                if j == 2:
                    dve.wait_ge(pe_k, 1)
                dve.tensor_copy(high, hT[:, slot]).then_inc(dve_hh, 1)
                dve.wait_ge(dve_hh, j + 1)
                dve.tensor_tensor(low, hT[:, slot], high.bitcast(F32), ALU.subtract).then_inc(dve_hl, 1)

            def keys(c):
                dve.wait_ge(act_qkv, 3 * c + 2)
                if c:
                    dve.wait_ge(pe_s, RT * c)
                for h in range(HG):
                    ins = dve.tensor_scalar(kx[:, h], kT[:], headmask[:, h:h + 1], None, ALU.mult)
                ins.then_inc(dve_kx, 1)

            def soft_max(c, r):
                dve.wait_ge(pe_s, RT * c + r + 1)
                s = b_s[r % 2][:].rearrange("p (q t) -> p q t", t=SEQ)
                link(dve.tensor_reduce(mx[:, r], s, AX_X, ALU.max))
                if c:
                    dve.wait_ge(pe_pT, RT * (c - 1) + r + 1)
                dve.tensor_tensor(prob[:, r].rearrange("p (q t) -> p q t", t=SEQ), s,
                                  mx[:, r].unsqueeze(2).broadcast_to([P, GROUPS * HG, SEQ]),
                                  ALU.subtract).then_inc(dve_dif, 1)

            def attend(c):
                dve.wait_ge(pe_sum, c + 1)
                link(dve.reciprocal(rsum[:], b_t[:, 0:GROUPS * HEADS]))
                if c:
                    dve.wait_ge(pe_aT, c)
                dve.tensor_tensor(att[:].rearrange("p g (n d) -> p (g n) d", d=HD),
                                  b_o[:].rearrange("p (q d) -> p q d", d=HD),
                                  rsum[:].unsqueeze(2).broadcast_to([P, GROUPS * HEADS, HD]),
                                  ALU.mult).then_inc(dve_att, 1)

            def residual(c):
                dve.wait_ge(pe_o, c + 1)
                dve.wait_ge(pool_yb, c + 1)
                dve.tensor_tensor(x1_tok[:, c], b_s1[:].rearrange("p (g h) -> p g h", h=D), y_tok[:, c],
                                  ALU.add).then_inc(dve_x1, 1)
                dve.wait_ge(dve_x1, c + 1)

            def ffn(c, i):
                k = FB * c + i
                dve.wait_ge(act_gel, k + 1)
                if i % 2 == 0:
                    dve.wait_ge(pe_wb, ROUTED * HALVES + E * c + i // 2 + 1)
                if k >= 2:
                    dve.wait_ge(pool_lo, k - 1)
                dve.tensor_tensor(pm[:, k % 2], gel[:, k % 2], b_w[:], ALU.mult).then_inc(dve_pm, 1)
                dve.wait_ge(dve_pm, k + 1)
                if k >= 2:
                    dve.wait_ge(pe_y, k - 1)
                dve.tensor_copy(p_h[:, k % 2], pm[:, k % 2]).then_inc(dve_ph, 1)

            def finish(c):
                dve.wait_ge(pe_yT, c + 1)
                dve.wait_ge(pool_xo, c + 1)
                dve.tensor_tensor(o_tok[:, c], b_o[:].rearrange("p (g h) -> p g h", h=D), x_tok[:, c],
                                  ALU.add).then_inc(dve_out, 1)

            for e in range(E):
                dve.memset(prio[:, e:e + 1], float(E - e)).then_inc(dve_const, 1)
            w_low(0)
            w_low(1)
            x_split(0)
            w_low(2)
            w_low(3)
            dve.wait_ge(pool_const, 2)
            for dst, src in ((sel_r, sel), (causal_r, causal[:])):
                dve.tensor_copy(dst[:], src).then_inc(dve_const, 1)
            dve.tensor_copy(ident_r[:], ident[0:SEQ, 0:SEQ].unsqueeze(1).broadcast_to([SEQ, GB, SEQ])
                            ).then_inc(dve_const, 1)
            dve.tensor_copy(selp_r[:].rearrange("k j (u m) -> k (j u) m", m=M), sel[:, :, 0:M]).then_inc(dve_const, 1)
            dve.tensor_reduce(headmask[:], head16[:].rearrange("p a h -> p h a"), AX_X, ALU.add).then_inc(dve_const, 1)
            dve.wait_ge(dve_const, E + 5)
            gate_up(0, 0)
            route(0)
            gate_up(0, 1)
            x_split(1)
            gate_up(0, 2)
            gate_up(0, 3)
            dve.wait_ge(act_proj, 1)
            dve.tensor_copy(qkT_h[:], projT[:, 0:2]).then_inc(dve_qk, 1)
            dve.wait_ge(dve_qk, 1)
            dve.tensor_tensor(qkT_l[:], projT[:, 0:2], qkT_h[:].bitcast(F32), ALU.subtract).then_inc(dve_qk, 1)
            gate_up(0, 4)
            dve.wait_ge(act_y, 1)
            norm(0, 0, y_tok[:, 0])
            gate_up(1, 0)
            route(1)
            norm_split(0, 0, hT_h[:, 0], hT_l[:, 0])
            gate_up(1, 1)
            gate_up(1, 2)
            keys(0)
            for r in range(RT):
                soft_max(0, r)
                if r < 2:
                    gate_up(1, 3 + r)
            attend(0)
            residual(0)
            norm(1, 1, x1_tok[:, 0])
            norm_split(1, 1, h2_h[:, 0], h2_l[:, 0])
            route(2)
            dve.wait_ge(act_y, 2)
            norm(2, 0, y_tok[:, 1])
            norm_split(2, 0, hT_h[:, 0], hT_l[:, 0])
            keys(1)
            for i in range(FB):
                ffn(0, i)
                if i < 4:
                    soft_max(1, i)
                if i == 9:
                    attend(1)
                if i == 11:
                    residual(1)
                    norm(3, 1, x1_tok[:, 1])
                if i == 12:
                    norm_split(3, 1, h2_h[:, 1], h2_l[:, 1])
            route(3)
            for i in range(FB):
                ffn(1, i)
                if i == 1:
                    finish(0)
            finish(1)

        @block.tensor
        def _(pe):
            def three(dst, wh, wl, xh, xl, first, last, before_low=None):
                pe.matmul(dst, wh, xh, start=first, stop=False)
                pe.matmul(dst, wl, xh, start=False, stop=False)
                if before_low:
                    pe.wait_ge(*before_low)
                return pe.matmul(dst, wh, xl, start=False, stop=last)

            def x_T(c):
                pe.wait_ge(ld_x[c], 16 * GB)
                for g in range(GROUPS):
                    ins = pe.transpose(b_s[c][:, g * P:(g + 1) * P], x_tok[:, c, g], ident[:])
                ins.then_inc(pe_x, 1)

            def block_up(c, n):
                k, j = CB * c + n, ORDER[n]
                if k < 2:
                    pe.wait_ge(dve_w, 2 * k + 2)
                if n == 0:
                    pe.wait_ge(dve_xh, c + 1)
                if k >= 1:
                    pe.wait_ge(act_g, k)
                three(b_h0[:], wgate_h[:, j], wgate_l[:, j], xT_h[:, c], xT_l[:, c], True, True,
                      (dve_x, c + 1) if n == 0 else None).then_inc(pe_g, 1)
                if k >= 1:
                    pe.wait_ge(dve_gu, k)
                three(b_h1[:], wup_h[:, j], wup_l[:, j], xT_h[:, c], xT_l[:, c], True, True).then_inc(pe_u, 1)

            def weights_up(c, n):
                k, j = ROUTED * c + n, ORDER[n + 1]
                if n == 0:
                    pe.wait_ge(act_gT, c + 1)
                else:
                    pe.wait_ge(act_wb, k)
                pe.matmul(b_w[:], selp_r[:, j], gT[:, 0], start=True, stop=True).then_inc(pe_wb, 1)

            def block_down(c, n):
                j = ORDER[n]
                if n == 0:
                    pe.wait_ge(dve_gu, CB * c + 1)
                    if c == 0:
                        pe.wait_ge(ld_down, 32)
                    else:
                        pe.wait_ge(act_y, c)
                else:
                    pe.wait_ge(pool_mid, ROUTED * c + n)
                src = gu[:, 0] if n == 0 else mid[:, (n - 1) % 2]
                for g in range(GROUPS):
                    ins = pe.matmul(b_y[:, g * D:(g + 1) * D], src[:, g * P:(g + 1) * P], wdown[:, j],
                                    start=(n == 0 and g == 0), stop=(n == CB - 1), skip_group_check=True)
                ins.then_inc(pe_down, 1)

            def cond_logits(c):
                if c == 0:
                    pe.wait_ge(act_cols, 3)
                else:
                    pe.wait_ge(act_wb, ROUTED * c)
                pe.wait_ge(act_x, c + 1)
                for g in range(GROUPS):
                    dst = b_w[:, g * E:(g + 1) * E]
                    pe.matmul(dst, xT[:, c, g * P:(g + 1) * P], cols[:, ROW_WT:ROW_WT + E], start=True, stop=False)
                    ins = pe.matmul(dst, cond4[:].rearrange("k b s -> k (b s)"), gcols[:, GROW_WG:GROWS],
                                    start=False, stop=True)
                ins.then_inc(pe_log, 1)

            def route_T(j):
                pe.wait_ge(dve_split, j + 1)
                for g in range(GROUPS):
                    ins = pe.transpose(b_w[0:2 * E, g * P:(g + 1) * P], wsplit[:, g].bitcast(F32), ident[:])
                ins.then_inc(pe_gT, 1)

            def norm_T(j, slot):
                pe.wait_ge(dve_hn, j + 1)
                if j == 0:
                    pe.wait_ge(act_cols, 3)
                elif j % 2 == 1:
                    pe.wait_ge(dve_att, j // 2 + 1)
                else:
                    pe.wait_ge(act_hT, j)
                for g in range(GROUPS):
                    ins = pe.transpose(b_t[:, g * P:(g + 1) * P], hn[:, slot, g], ident[:])
                ins.then_inc(pe_hT, 1)

            def qkv(c):
                pe.wait_ge(dve_qk, 2)
                pe.wait_ge(dve_hh, 2 * c + 1)
                if c == 0:
                    pe.wait_ge(act_x, 2)
                else:
                    pe.wait_ge(dve_x1, c)
                three(b_s0[:], qkT_h[:, 0], qkT_l[:, 0], hT_h[:, 0], hT_l[:, 0], True, True,
                      (dve_hl, 2 * c + 1)).then_inc(pe_q, 1)
                three(b_s1[:], qkT_h[:, 1], qkT_l[:, 1], hT_h[:, 0], hT_l[:, 0], True, True).then_inc(pe_k, 1)
                wv = projT[:, 2].rearrange("p (r h d) -> p h r d", r=RT, h=HG)
                for b in range(NB):
                    for h in range(HG):
                        ins = pe.matmul(b_t[h * SEQ:(h + 1) * SEQ, b * RT * HD:(b + 1) * RT * HD],
                                        hT[:, 0, b * SEQ:(b + 1) * SEQ], wv[:, h], start=True, stop=True)
                ins.then_inc(pe_v, 1)

            def scores(c, r):
                if r == 0:
                    pe.wait_ge(act_qkv, 3 * c + 2)
                    pe.wait_ge(dve_kx, c + 1)
                elif r >= 2:
                    pe.wait_ge(dve_dif, RT * c + r - 1)
                dst = b_s[r % 2]
                pe.matmul(dst[:], ident_r[:].rearrange("k b s -> k (b s)"),
                          causal_r[:].unsqueeze(1).broadcast_to([SEQ, GROUPS * HG, SEQ]),
                          start=True, stop=False, skip_group_check=True)
                ch = slice(r * HG * HD, (r + 1) * HG * HD)
                for g in range(GROUPS):
                    for b in range(GB):
                        col = (g * GB + b) * SEQ
                        ins = pe.matmul(dst[b * SEQ:(b + 1) * SEQ, g * HG * SEQ:(g + 1) * HG * SEQ],
                                        qT[ch, col:col + SEQ], kx[ch, :, col:col + SEQ],
                                        start=False, stop=True, skip_group_check=True)
                ins.then_inc(pe_s, 1)

            def prob_T(c, r):
                pe.wait_ge(act_exp, RT * c + r + 1)
                if r == 0:
                    pe.wait_ge(act_qkv, 3 * c + 3)
                else:
                    pe.wait_ge(act_pT, RT * c + r)
                for g in range(GROUPS):
                    ins = pe.transpose(b_t[:, g * P:(g + 1) * P], prob[:, r, g * P:(g + 1) * P], ident[:])
                ins.then_inc(pe_pT, 1)

            def values(c, r):
                pe.wait_ge(act_pT, RT * c + r + 1)
                if r == 0:
                    pe.wait_ge(pool_vx, c + 1)
                    pe.wait_ge(act_proj, 1)
                w = HG * HD
                for g in range(GROUPS):
                    for b in range(GB):
                        q = g * GB + b
                        ins = pe.matmul(b_o[b * SEQ:(b + 1) * SEQ, g * D + r * w:g * D + (r + 1) * w],
                                        probT[:, r, q * SEQ:(q + 1) * SEQ], vx[:, q, r], start=True, stop=True)
                ins.then_inc(pe_pv, 1)

            def sums(c):
                for g in range(GROUPS):
                    for r in range(RT):
                        at = g * HEADS + r * HG
                        ins = pe.matmul(b_t[:, at:at + HG], probT[:, r, g * P:(g + 1) * P], vmask[:, :, 0],
                                        start=True, stop=True)
                ins.then_inc(pe_sum, 1)

            def project(c):
                pe.wait_ge(dve_att, c + 1)
                for g in range(GROUPS):
                    ins = pe.transpose(b_s0[:, g * P:(g + 1) * P], att[:, g], ident[:])
                ins.then_inc(pe_aT, 1)
                pe.wait_ge(act_aT, c + 1)
                for g in range(GROUPS):
                    ins = pe.matmul(b_s1[:, g * D:(g + 1) * D], attT[:, g * P:(g + 1) * P], projT[:, 3],
                                    start=True, stop=True)
                ins.then_inc(pe_o, 1)

            def ffn_logits(c):
                pe.wait_ge(act_hT, 2 * c + 2)
                if c == 0:
                    pe.wait_ge(act_wb, ROUTED * HALVES)
                else:
                    pe.wait_ge(dve_pm, FB * c)
                for g in range(GROUPS):
                    ins = pe.matmul(b_w[:, g * E:(g + 1) * E], hT[:, 1, g * P:(g + 1) * P],
                                    cols[:, ROW_ROUTER:ROW_ROUTER + E], start=True, stop=True)
                ins.then_inc(pe_log, 1)

            def ffn_up(c, i):
                k = FB * c + i
                if c == 0:
                    if i % 4 == 0:
                        pe.wait_ge(pool_w1, i // 4 + 1)
                if i == 0:
                    pe.wait_ge(dve_hh, 2 * c + 2)
                    if c == 0:
                        pe.wait_ge(act_g, CB * HALVES)
                        pe.wait_ge(dve_gu, CB * HALVES)
                if k >= 2:
                    pe.wait_ge(act_gel, k - 1)
                three(b_h[i % 2][:], w1_h[:, i], w1_l[:, i], h2_h[:, c], h2_l[:, c], True, True,
                      (dve_hl, 2 * c + 2) if i == 0 else None).then_inc(pe_h, 1)

            def ffn_weights(c, e):
                if e == 0:
                    pe.wait_ge(act_gT, HALVES + c + 1)
                else:
                    pe.wait_ge(dve_pm, FB * c + 2 * e)
                pe.matmul(b_w[:], sel_r[:, e], gT[:, 1], start=True, stop=True).then_inc(pe_wb, 1)

            def ffn_down(c, i):
                k = FB * c + i
                pe.wait_ge(dve_ph, k + 1)
                if c == 0 and i % 4 == 0:
                    pe.wait_ge(pool_w2, i // 4 + 1)
                if i == 0:
                    pe.wait_ge(*((act_y, HALVES) if c == 0 else (act_yT, c)))
                three(b_y[:], w2_h[:, i], w2_l[:, i], p_h[:, k % 2], p_l[:, k % 2], i == 0, i == FB - 1,
                      (pool_lo, k + 1)).then_inc(pe_y, 1)

            def y_T(c):
                pe.wait_ge(act_yT, c + 1)
                pe.wait_ge(dve_att, HALVES)
                if c:
                    pe.wait_ge(dve_out, c)
                for g in range(GROUPS):
                    ins = pe.transpose(b_o[:, g * P:(g + 1) * P], yT[:, g * P:(g + 1) * P], ident[:])
                ins.then_inc(pe_yT, 1)

            pe.wait_ge(pool_const, 1)
            x_T(0)
            pe.wait_ge(ld_rows, 7 * 16)
            pe.wait_ge(ld_cond, 2 * 16)
            pe.transpose(b_t[:, 0:ROWS], rows[:], ident[0:ROWS, 0:ROWS])
            pe.transpose(b_t[0:M, ROWS:ROWS + GROWS], grows[:], ident[0:GROWS, 0:GROWS]).then_inc(pe_cols, 1)
            block_up(0, 0)
            cond_logits(0)
            block_up(0, 1)
            block_down(0, 0)
            x_T(1)
            pe.wait_ge(ld_proj, 3 * 16)
            for k in range(4):
                ins = pe.transpose(b_o[:, k * P:(k + 1) * P], proj[:, k], ident[:])
            ins.then_inc(pe_proj, 1)
            route_T(0)
            weights_up(0, 0)
            for n in range(1, ROUTED):
                block_up(0, n + 1)
                weights_up(0, n)
                block_down(0, n)
            block_down(0, ROUTED)
            block_up(1, 0)
            cond_logits(1)
            norm_T(0, 0)
            block_up(1, 1)
            block_down(1, 0)
            route_T(1)
            weights_up(1, 0)
            qkv(0)
            block_up(1, 2)
            block_down(1, 1)
            for r in range(RT):
                scores(0, r)
                if r < 3:
                    weights_up(1, r + 1)
                if r < 2:
                    block_up(1, r + 3)
                prob_T(0, r)
                if r < 3:
                    block_down(1, r + 2)
                values(0, r)
            sums(0)
            project(0)
            norm_T(1, 1)
            ffn_logits(0)
            ffn_up(0, 0)
            ffn_up(0, 1)
            norm_T(2, 0)
            route_T(2)
            ffn_weights(0, 0)
            qkv(1)
            scores(1, 0)
            scores(1, 1)
            for i in range(2, FB + 2):
                if i < FB:
                    ffn_up(0, i)
                    if i % 2 == 0:
                        ffn_weights(0, i // 2)
                ffn_down(0, i - 2)
                if i in (2, 3):
                    scores(1, i)
                if 5 <= i < 9:
                    prob_T(1, i - 5)
                if 6 <= i < 10:
                    values(1, i - 6)
                if i == 9:
                    sums(1)
                if i == 11:
                    project(1)
                if i == 13:
                    norm_T(3, 1)
            ffn_logits(1)
            ffn_up(1, 0)
            ffn_up(1, 1)
            route_T(3)
            ffn_weights(1, 0)
            y_T(0)
            for i in range(2, FB + 2):
                if i < FB:
                    ffn_up(1, i)
                    if i % 2 == 0:
                        ffn_weights(1, i // 2)
                ffn_down(1, i - 2)
            y_T(1)


_INS = ['x', 'cond_64', 'L0_cond_wt', 'L0_cond_wg', 'L0_cond_w_gate', 'L0_cond_w_up', 'L0_cond_w_down',
        'L0_cond_sw_gate', 'L0_cond_sw_up', 'L0_cond_sw_down', 'L0_ffn_ln1_w', 'L0_ffn_ln1_b',
        'L0_ffn_in_proj_w', 'L0_ffn_in_proj_b', 'L0_ffn_out_proj_w', 'L0_ffn_out_proj_b', 'L0_ffn_ln2_w',
        'L0_ffn_ln2_b', 'L0_ffn_router_w', 'L0_ffn_w1', 'L0_ffn_w2']


def kernel(**inputs):
    import numpy as _np
    import concourse.bacc as _bacc
    from concourse import mybir as _mybir
    from concourse.bass_utils import run_bass_kernel_spmd as _run

    nc = _bacc.Bacc("TRN2", target_bir_lowering=False, num_devices=1)
    arrays, args = {}, []
    for name in _INS:
        a = _np.ascontiguousarray(inputs[name])
        arrays[f"in_{name}"] = a
        args.append(nc.dram_tensor(f"in_{name}", a.shape, _mybir.dt.from_np(a.dtype), kind="ExternalInput").ap())
    shape = inputs['x'].shape
    args.append(nc.dram_tensor("out_0", shape, _mybir.dt.float32, kind="ExternalOutput").ap())
    build(nc, *args)
    r = _run(nc, [arrays], core_ids=[0])
    return r.results[0]["out_0"]
```

```python
from contextlib import ExitStack

import concourse.bass as bass
from concourse import mybir

F32 = mybir.dt.float32
F32R = mybir.dt.float32r
I32 = mybir.dt.int32
U32 = mybir.dt.uint32
ALU = mybir.AluOpType
ACT = mybir.ActivationFunctionType
AX_X = mybir.AxisListType.X

P = 128
HALVES = 2
BATCH = 32
SEQ = 32
D = 128
GROUPS = 4
GB = 4
N = GROUPS * P
NB = GROUPS * GB
E = 8
M = 64
CB = E * M // P + 1
ROUTED = CB - 1
SHARED = CB - 1
F = 256
FB = E * F // P
LAG = 3
HEADS = 16
HD = D // HEADS
HG = 4
RT = HEADS // HG
EPS = 1e-5
LEAK = 0.01
MASKED = -1e30
RSQRT_SEED = 0x5F3759DF

ROW_BQ, ROW_BK, ROW_BV, ROW_LN1W, ROW_LN1B, ROW_LN2W, ROW_LN2B = range(7)
ROW_WT, ROW_ROUTER, ROWS = 7, 15, 23
GROW_WG, GROWS = 32, 40


def build(nc, x, cond, wt, wg, w_gate, w_up, w_down, sw_gate, sw_up, sw_down, ln1_w, ln1_b, in_w, in_b,
          out_w, out_b, ln2_w, ln2_b, router_w, w1, w2, out):
    with ExitStack() as ctx:
        def sb(name, shape, dt=F32):
            return ctx.enter_context(nc.sbuf_tensor(name, shape, dt))

        def bank(name):
            return ctx.enter_context(nc.psum_tensor(name, [P, N], F32))

        def sem(name):
            return ctx.enter_context(nc.semaphore(name))

        b_h0 = bank("b_h0")
        b_h1 = bank("b_h1")
        b_w = bank("b_w")
        b_y = bank("b_y")
        b_s0 = bank("b_s0")
        b_s1 = bank("b_s1")
        b_t = bank("b_t")
        b_o = bank("b_o")
        b_s = [b_s0, b_s1]
        b_h = [[b_h0, b_h1], [b_h0, b_h1, b_s0, b_s1]]
        b_we = [[b_w], [b_w, b_t]]
        b_rt = [b_w, b_w, b_w, b_s0]

        x_tok = sb("x_tok", [P, HALVES, GROUPS, D])
        rows = sb("rows", [ROWS, D])
        grows = sb("grows", [GROWS, D])
        cols = sb("cols", [P, ROWS])
        gcols = sb("gcols", [P, GROWS])
        cond4 = sb("cond4", [P, GB, SEQ])
        bias_k = sb("bias_k", [P, HG])
        wgate = sb("wgate", [P, CB, P])
        wup = sb("wup", [P, CB, P])
        wdown = sb("wdown", [P, CB, D])
        wgate_h, wgate_l = sb("wgate_h", [P, CB, P], F32R), sb("wgate_l", [P, CB, P], F32R)
        wup_h, wup_l = sb("wup_h", [P, CB, P], F32R), sb("wup_l", [P, CB, P], F32R)
        proj = sb("proj", [P, 4, D])
        projT = sb("projT", [P, 4, D])
        qkT_h, qkT_l = sb("qkT_h", [P, 2, D], F32R), sb("qkT_l", [P, 2, D], F32R)
        bo = sb("bo", [P, D])
        w1_s = sb("w1_s", [P, FB, P])
        w2_s = sb("w2_s", [P, FB, D])
        w1_h, w1_l = sb("w1_h", [P, FB, P], F32R), sb("w1_l", [P, FB, P], F32R)
        w2_h, w2_l = sb("w2_h", [P, FB, D], F32R), sb("w2_l", [P, FB, D], F32R)

        ident = sb("ident", [P, P])
        ident_r = sb("ident_r", [SEQ, GB, SEQ], F32R)
        causal = sb("causal", [SEQ, SEQ])
        causal_r = sb("causal_r", [SEQ, SEQ], F32R)
        head16 = sb("head16", [P, RT, HG])
        headmask = sb("headmask", [P, HG])
        vmask = sb("vmask", [P, HG, HD])
        sel_r = sb("sel_r", [2 * E, E, P], F32R)
        selp_r = sb("selp_r", [2 * E, ROUTED, P], F32R)
        expert = sb("expert", [P, E])

        xT = sb("xT", [P, HALVES, N])
        xT_h, xT_l = sb("xT_h", [P, HALVES, N], F32R), sb("xT_l", [P, HALVES, N], F32R)
        gate_s = sb("gate_s", [P, 2, N])
        leaky = sb("leaky", [P, 2, N])
        gu = sb("gu", [P, 2, N])
        wb_s = sb("wb_s", [P, 2, N])
        mid = sb("mid", [P, 2, N])
        y_tok = sb("y_tok", [P, HALVES, GROUPS, D])
        hn = sb("hn", [P, 2, GROUPS, D])
        hT = sb("hT", [P, 2, N])
        hT_h, hT_l = sb("hT_h", [P, N], F32R), sb("hT_l", [P, N], F32R)
        h2_h, h2_l = sb("h2_h", [P, HALVES, N], F32R), sb("h2_l", [P, HALVES, N], F32R)
        qT = sb("qT", [P, N])
        kx = sb("kx", [P, HG, N])
        vc = sb("vc", [P, NB, RT, HD])
        vx = sb("vx", [P, NB, RT, HG, HD])
        mx = sb("mx", [P, RT, GROUPS * HG])
        prob = sb("prob", [P, RT, N])
        sel = prob[0:2 * E, 0:2].rearrange("k r (e p) -> k (r e) p", p=P)
        probT = sb("probT", [P, RT, N])
        psum = sb("psum", [P, GROUPS, RT, HG])
        rsum = sb("rsum", [P, GROUPS * HEADS])
        att = wup[:, 0:GROUPS]
        attT = wgate[:, 0:GROUPS].rearrange("p g q -> p (g q)")
        x1_tok = sb("x1_tok", [P, HALVES, GROUPS, D])
        p_h, p_l = sb("p_h", [P, LAG, N], F32R), sb("p_l", [P, LAG, N], F32R)
        gel = w1_s[:, 0:FB // 2].rearrange("p (s b) q -> p s (b q)", s=2)
        pm = w1_s[:, FB // 2:FB].rearrange("p (s b) q -> p s (b q)", s=2)
        yT = w2_s[:, 0:GROUPS].rearrange("p b q -> p (b q)")
        o_tok = w2_s[:, GROUPS:3 * GROUPS].rearrange("p (c g) h -> p c g h", c=HALVES)
        stat6 = sb("stat6", [P, GROUPS, 6])
        stat2 = sb("stat2", [P, GROUPS, 2])
        lnw = sb("lnw", [P, 3, GROUPS])
        top = sb("top", [P, GROUPS, E])
        topi = sb("topi", [P, GROUPS, E], U32)
        rt = sb("rt", [P, 5, GROUPS, E])
        rs = sb("rs", [P, 4, GROUPS])
        expo = sb("expo", [P, GROUPS, E])
        wsplit = sb("wsplit", [P, GROUPS, 2 * E], F32R)
        gT = sb("gT", [2 * E, 2, N], F32R)

        ld_x = [sem("ld_x0"), sem("ld_x1")]
        ld_rows, ld_cond, ld_shared, ld_gate, ld_up, ld_down, ld_proj, ld_w1, ld_w2 = (
            sem(s) for s in ("ld_rows", "ld_cond", "ld_shared", "ld_gate", "ld_up", "ld_down", "ld_proj",
                             "ld_w1", "ld_w2"))
        pool_const, pool_chain, pool_mid, pool_yb, pool_vx, pool_xo, pool_lo, pool_w1, pool_w2 = (
            sem(s) for s in ("pool_const", "pool_chain", "pool_mid", "pool_yb", "pool_vx", "pool_xo",
                             "pool_lo", "pool_w1", "pool_w2"))
        act_cols, act_x, act_proj, act_g, act_wb, act_gT, act_y, act_hT, act_qk, act_exp, act_pT = (
            sem(s) for s in ("act_cols", "act_x", "act_proj", "act_g", "act_wb", "act_gT", "act_y", "act_hT",
                             "act_qk", "act_exp", "act_pT"))
        act_aT, act_re, act_gel, act_yT, act_w1, act_w2, act_wh = (
            sem(s) for s in ("act_aT", "act_re", "act_gel", "act_yT", "act_w1", "act_w2", "act_wh"))
        dve_chain, dve_const, dve_xh, dve_x, dve_w, dve_gu, dve_split, dve_ld, dve_hn = (
            sem(s) for s in ("dve_chain", "dve_const", "dve_xh", "dve_x", "dve_w", "dve_gu", "dve_split",
                             "dve_ld", "dve_hn"))
        dve_hh, dve_hl, dve_kx, dve_dif, dve_att, dve_x1, dve_pm, dve_ph, dve_out, dve_qk = (
            sem(s) for s in ("dve_hh", "dve_hl", "dve_kx", "dve_dif", "dve_att", "dve_x1", "dve_pm", "dve_ph",
                             "dve_out", "dve_qk"))
        pe_x, pe_cols, pe_proj, pe_g, pe_u, pe_wb, pe_down, pe_log, pe_gT, pe_hT = (
            sem(s) for s in ("pe_x", "pe_cols", "pe_proj", "pe_g", "pe_u", "pe_wb", "pe_down", "pe_log",
                             "pe_gT", "pe_hT"))
        pe_q, pe_k, pe_v, pe_s, pe_pT, pe_pv, pe_sum, pe_aT, pe_o, pe_h, pe_y, pe_yT = (
            sem(s) for s in ("pe_q", "pe_k", "pe_v", "pe_s", "pe_pT", "pe_pv", "pe_sum", "pe_aT", "pe_o",
                             "pe_h", "pe_y", "pe_yT"))
        act_v, dve_sum = sem("act_v"), sem("dve_sum")
        st_out = sem("st_out")

        GT_SLOT = [0, 0, 1, 0]
        ORDER = [SHARED, 0, 1, 2, 3]
        block = ctx.enter_context(nc.Block())

        def tile_rows(ap, c, b):
            return ap.rearrange("s (c g b) h -> c b s g h", c=HALVES, g=GROUPS)[c, b]

        @block.sync
        def _(sp):
            for b in range(GB):
                sp.dma_start(x_tok[b * SEQ:(b + 1) * SEQ, 0], tile_rows(x, 0, b)).then_inc(ld_x[0], 16)
            sp.dma_start(wgate[:, SHARED, :], sw_gate).then_inc(ld_shared, 16)
            sp.dma_start(wup[:, SHARED, :], sw_up).then_inc(ld_shared, 16)
            sp.dma_start(wgate[:, 0:SHARED, :].rearrange("h j (u m) -> h (j u) m", m=M),
                         w_gate.rearrange("e h m -> h e m")).then_inc(ld_gate, 16)
            sp.dma_start(wup[:, 0:SHARED, :].rearrange("h j (u m) -> h (j u) m", m=M),
                         w_up.rearrange("e h m -> h e m")).then_inc(ld_up, 16)
            sp.dma_start(wdown[:, 0:SHARED, :],
                         w_down.rearrange("e m h -> (e m) h").rearrange("(j p) h -> p j h", p=P)).then_inc(ld_down, 16)
            sp.dma_start(wdown[:, SHARED, :], sw_down).then_inc(ld_down, 16)
            for b in range(GB):
                sp.dma_start(x_tok[b * SEQ:(b + 1) * SEQ, 1], tile_rows(x, 1, b)).then_inc(ld_x[1], 16)
            sp.dma_start(proj[:, 0:3, :], in_w.rearrange("(k p) h -> p k h", p=P)).then_inc(ld_proj, 16)
            sp.dma_start(proj[:, 3, :], out_w).then_inc(ld_proj, 16)
            sp.dma_start(bo[:], out_b.partition_broadcast(P)).then_inc(ld_proj, 16)
            sp.dma_start(w1_s[:].rearrange("h (e b) p -> h e (b p)", e=E),
                         w1.rearrange("e h f -> h e f")).then_inc(ld_w1, 16)
            sp.dma_start(w2_s[:], w2.rearrange("e (b p) h -> p (e b) h", p=P)).then_inc(ld_w2, 16)
            for c in range(HALVES):
                sp.wait_ge(dve_out, c + 1)
                for b in range(GB):
                    sp.dma_start(tile_rows(out, c, b), o_tok[b * SEQ:(b + 1) * SEQ, c]).then_inc(st_out, 16)
            sp.wait_ge(st_out, 16 * GB * HALVES)

        @block.gpsimd
        def _(pool):
            chain = [0]

            def link(ins):
                chain[0] += 1
                ins.then_inc(pool_chain, 1)
                pool.wait_ge(pool_chain, chain[0])

            link(pool.memset(ident[:], 0.0))
            pool.affine_select(out=ident[:], in_=ident[:], compare_op=ALU.not_equal, fill=1.0, base=0,
                               pattern=[[-1, P]], channel_multiplier=1).then_inc(pool_const, 1)
            pool.memset(grows[:, M:D], 0.0).then_inc(pool_const, 1)
            link(pool.memset(sel, 0.0))
            for part in range(2):
                link(pool.affine_select(out=sel, in_=sel, compare_op=ALU.not_equal, fill=1.0, base=-E * part,
                                        pattern=[[-1, E], [0, P]], channel_multiplier=1))
            link(pool.memset(causal[:], 0.0))
            link(pool.affine_select(out=causal[:], in_=causal[:], compare_op=ALU.is_ge, fill=MASKED, base=0,
                                    pattern=[[-1, SEQ]], channel_multiplier=1))
            link(pool.memset(head16[:], 1.0))
            link(pool.affine_select(out=head16[:], in_=head16[:], compare_op=ALU.is_ge, fill=0.0, base=0,
                                    pattern=[[-SEQ, RT], [-HD, HG]], channel_multiplier=1))
            link(pool.affine_select(out=head16[:], in_=head16[:], compare_op=ALU.is_ge, fill=0.0, base=HD - 1,
                                    pattern=[[SEQ, RT], [HD, HG]], channel_multiplier=-1))
            link(pool.memset(vmask[:], 1.0))
            link(pool.affine_select(out=vmask[:], in_=vmask[:], compare_op=ALU.is_ge, fill=0.0, base=0,
                                    pattern=[[-SEQ, HG], [0, HD]], channel_multiplier=1))
            pool.affine_select(out=vmask[:], in_=vmask[:], compare_op=ALU.is_ge, fill=0.0, base=SEQ - 1,
                               pattern=[[SEQ, HG], [0, HD]], channel_multiplier=-1).then_inc(pool_const, 1)

            def mids(c, n):
                k, s = ROUTED * c + n, n % 2
                pool.wait_ge(dve_gu, CB * c + n + 2)
                pool.wait_ge(act_wb, k + 1)
                if k >= 2:
                    pool.wait_ge(pe_down, CB * (c if n >= 2 else c - 1) + (n if n >= 2 else n + 4))
                pool.tensor_tensor(mid[:, s], gu[:, (n + 1) % 2], wb_s[:, s], ALU.mult).then_inc(pool_mid, 1)

            def residual_bias(c):
                pool.wait_ge(act_y, c + 1)
                if c == 0:
                    pool.wait_ge(ld_proj, 48)
                pool.wait_ge(dve_hn, c + 1)
                pool.tensor_tensor(y_tok[:, c], y_tok[:, c], bo[:].unsqueeze(1).broadcast_to([P, GROUPS, D]),
                                   ALU.add).then_inc(pool_yb, 1)

            def spread_values(c):
                pool.wait_ge(act_v, c + 1)
                if c:
                    pool.wait_ge(pe_pv, RT * c)
                v = vc[:].rearrange("p b r d -> p (b r) d").unsqueeze(2).broadcast_to([P, NB * RT, HG, HD])
                pool.tensor_tensor(vx[:].rearrange("p b r h d -> p (b r) h d"), v,
                                   vmask[:].unsqueeze(1).broadcast_to([P, NB * RT, HG, HD]),
                                   ALU.mult).then_inc(pool_vx, 1)

            def residual_in(c):
                pool.wait_ge(dve_x1, c + 1)
                pool.tensor_tensor(x_tok[:, c], x_tok[:, c], x1_tok[:, c], ALU.add).then_inc(pool_xo, 1)

            def ffn_low(c, i):
                k = FB * c + i
                pool.wait_ge(dve_ph, k + 1)
                if k >= LAG:
                    pool.wait_ge(pe_y, k - LAG + 1)
                pool.tensor_tensor(p_l[:, k % LAG], pm[:, k % 2], p_h[:, k % LAG].bitcast(F32),
                                   ALU.subtract).then_inc(pool_lo, 1)

            def weight_low(which, i):
                full, high, low, src, dst = ((w1_s, w1_h, w1_l, act_w1, pool_w1), (w2_s, w2_h, w2_l, act_w2, pool_w2))[which]
                pool.wait_ge(src, i + 1)
                b = slice(4 * i, 4 * i + 4)
                pool.tensor_tensor(low[:, b], full[:, b], high[:, b].bitcast(F32), ALU.subtract).then_inc(dst, 1)

            for n in range(ROUTED):
                weight_low(0, n)
                mids(0, n)
            residual_bias(0)
            for n in range(ROUTED):
                mids(1, n)
                if n == 0:
                    spread_values(0)
                else:
                    weight_low(1, n - 1)
            weight_low(1, ROUTED - 1)
            residual_bias(1)
            residual_in(0)
            spread_values(1)
            for i in range(FB):
                ffn_low(0, i)
            residual_in(1)
            for i in range(FB):
                ffn_low(1, i)

        @block.scalar
        def _(act):
            for at, src in ((ROW_BQ, in_b.rearrange("(k h) -> k h", k=3)), (ROW_LN1W, ln1_w.unsqueeze(0)),
                            (ROW_LN1B, ln1_b.unsqueeze(0)), (ROW_LN2W, ln2_w.unsqueeze(0)),
                            (ROW_LN2B, ln2_b.unsqueeze(0)), (ROW_WT, wt), (ROW_ROUTER, router_w)):
                act.dma_start(rows[at:at + src.shape[0], :], src).then_inc(ld_rows, 16)
            act.dma_start(grows[0:GROW_WG, 0:M], cond).then_inc(ld_cond, 16)
            act.dma_start(grows[GROW_WG:GROWS, 0:M], wg).then_inc(ld_cond, 16)

            def x_in(c):
                act.wait_ge(pe_x, c + 1)
                nc.scalar.copy(xT[:, c], b_s[c][:]).then_inc(act_x, 1)

            def gate_copy(c, n):
                k = CB * c + n
                act.wait_ge(pe_g, k + 1)
                if k >= 2:
                    act.wait_ge(dve_gu, k - 1)
                nc.scalar.copy(gate_s[:, k % 2], b_h0[:]).then_inc(act_g, 1)

            def weights_copy(c, n):
                k = ROUTED * c + n
                act.wait_ge(pe_wb, k + 1)
                if k >= 2:
                    act.wait_ge(pool_mid, k - 1)
                nc.scalar.copy(wb_s[:, n % 2], b_w[:]).then_inc(act_wb, 1)

            def route_exp(j, scale):
                act.wait_ge(dve_ld, j + 1)
                nc.scalar.activation(expo[:], rt[:, 0], ACT.Exp, scale=scale).then_inc(act_re, 1)

            def route_T(j):
                act.wait_ge(pe_gT, j + 1)
                nc.scalar.copy(gT[:, GT_SLOT[j]], b_rt[j][0:2 * E, :]).then_inc(act_gT, 1)

            def y_copy(c):
                act.wait_ge(pe_down, CB * (c + 1))
                nc.scalar.copy(y_tok[:, c].rearrange("p g h -> p (g h)"), b_y[:]).then_inc(act_y, 1)

            def norm_T(j):
                slot = j // HALVES
                w, b = ((ROW_LN1W, ROW_LN1B), (ROW_LN2W, ROW_LN2B))[slot]
                act.wait_ge(pe_hT, j + 1)
                if j % HALVES:
                    act.wait_ge(dve_hl, j)
                    act.wait_ge(*((pe_v, 1) if slot == 0 else (pe_log, 3)))
                nc.scalar.activation(hT[:, slot], b_t[:], ACT.Identity, scale=cols[:, w:w + 1],
                                     bias=cols[:, b:b + 1]).then_inc(act_hT, 1)

            def qk_copy(c):
                act.wait_ge(pe_q, c + 1)
                if c:
                    act.wait_ge(pe_s, RT * c)
                nc.scalar.activation(qT[:], b_s0[:], ACT.Identity, scale=1.0,
                                     bias=cols[:, ROW_BQ:ROW_BQ + 1])
                act.wait_ge(pe_k, c + 1)
                for h in range(HG):
                    ins = nc.scalar.activation(kx[:, h], b_s1[:], ACT.Identity, scale=headmask[:, h:h + 1],
                                               bias=bias_k[:, h:h + 1])
                ins.then_inc(act_qk, 1)

            def v_copy(c):
                act.wait_ge(pe_v, c + 1)
                if c:
                    act.wait_ge(pool_vx, c)
                nc.scalar.copy(vc[:].rearrange("p b r d -> p (b r d)"), b_t[:]).then_inc(act_v, 1)

            def soft_exp(c, r):
                act.wait_ge(dve_dif, RT * c + r + 1)
                nc.scalar.activation(prob[:, r], prob[:, r], ACT.Exp, scale=HD ** -0.5).then_inc(act_exp, 1)

            def prob_T(c, r):
                act.wait_ge(pe_pT, RT * c + r + 1)
                if c:
                    act.wait_ge(pe_pv, RT * c)
                nc.scalar.copy(probT[:, r], b_t[:]).then_inc(act_pT, 1)

            def att_T(c):
                act.wait_ge(pe_aT, c + 1)
                if c:
                    act.wait_ge(pe_o, c)
                nc.scalar.activation(attT, b_s0[:], ACT.Identity, scale=1.0,
                                     bias=cols[:, ROW_BV:ROW_BV + 1]).then_inc(act_aT, 1)

            def gelu(c, i):
                k = FB * c + i
                act.wait_ge(pe_h, k + 1)
                if k == 0:
                    act.wait_ge(pool_w1, FB // 4)
                if k >= 2:
                    act.wait_ge(dve_pm, k - 1)
                nc.scalar.activation(gel[:, k % 2], b_h[c][i % len(b_h[c])][:], ACT.Gelu).then_inc(act_gel, 1)

            def y_out(c):
                act.wait_ge(pe_y, FB * (c + 1))
                if c:
                    act.wait_ge(pe_yT, c)
                nc.scalar.copy(yT[:], b_y[:]).then_inc(act_yT, 1)

            act.wait_ge(ld_shared, 32)
            for high, full in ((wgate_h, wgate), (wup_h, wup)):
                nc.scalar.copy(high[:, SHARED], full[:, SHARED]).then_inc(act_wh, 1)
            x_in(0)
            for high, full, ld in ((wgate_h, wgate, ld_gate), (wup_h, wup, ld_up)):
                act.wait_ge(ld, 16)
                nc.scalar.copy(high[:, 0:SHARED], full[:, 0:SHARED]).then_inc(act_wh, 1)
            act.wait_ge(pe_cols, 1)
            nc.scalar.copy(cols[:], b_t[:, 0:ROWS]).then_inc(act_cols, 1)
            nc.scalar.copy(gcols[:], b_t[:, ROWS:ROWS + GROWS]).then_inc(act_cols, 1)
            nc.scalar.copy(cond4[:], b_t[:, ROWS:ROWS + GROW_WG].unsqueeze(1).broadcast_to([P, GB, SEQ])
                           ).then_inc(act_cols, 1)
            def w_high(which, i):
                high, full, ld, done = ((w1_h, w1_s, ld_w1, act_w1), (w2_h, w2_s, ld_w2, act_w2))[which]
                if i == 0:
                    act.wait_ge(ld, 16)
                nc.scalar.copy(high[:, 4 * i:4 * i + 4], full[:, 4 * i:4 * i + 4]).then_inc(done, 1)

            gate_copy(0, 0)
            route_exp(0, 0.5)
            gate_copy(0, 1)
            x_in(1)
            act.wait_ge(pe_proj, 1)
            nc.scalar.copy(projT[:].rearrange("p k h -> p (k h)"), b_o[:]).then_inc(act_proj, 1)
            gate_copy(0, 2)
            for i in range(FB // 4):
                w_high(0, i)
            route_T(0)
            for n in range(ROUTED):
                weights_copy(0, n)
                if n + 3 < CB:
                    gate_copy(0, n + 3)
            y_copy(0)
            gate_copy(1, 0)
            norm_T(0)
            route_exp(1, 0.5)
            gate_copy(1, 1)
            qk_copy(0)
            v_copy(0)
            route_T(1)
            weights_copy(1, 0)
            gate_copy(1, 2)
            for i in range(FB // 4):
                w_high(1, i)
            for r in range(RT):
                soft_exp(0, r)
                if r < 3:
                    weights_copy(1, r + 1)
                prob_T(0, r)
                if r < 2:
                    gate_copy(1, r + 3)
            y_copy(1)
            norm_T(1)
            att_T(0)
            qk_copy(1)
            norm_T(2)
            v_copy(1)
            route_exp(2, 1.0)
            for r in range(RT):
                soft_exp(1, r)
                if r == 1:
                    route_T(2)
            for i in range(FB):
                gelu(0, i)
                if 1 <= i < 5:
                    prob_T(1, i - 1)
                if i == 7:
                    att_T(1)
                if i == 12:
                    norm_T(3)
            route_exp(3, 1.0)
            gelu(1, 0)
            route_T(3)
            y_out(0)
            for i in range(1, FB):
                gelu(1, i)
            y_out(1)

        @block.vector
        def _(dve):
            chain = [0]

            def link(ins):
                chain[0] += 1
                ins.then_inc(dve_chain, 1)
                dve.wait_ge(dve_chain, chain[0])

            def x_split(c):
                dve.wait_ge(act_x, c + 1)
                dve.tensor_copy(xT_h[:, c], xT[:, c]).then_inc(dve_xh, 1)
                dve.wait_ge(dve_xh, c + 1)
                dve.tensor_tensor(xT_l[:, c], xT[:, c], xT_h[:, c].bitcast(F32), ALU.subtract).then_inc(dve_x, 1)

            def w_low(i):
                full, high, low, b = ((wgate, wgate_h, wgate_l, slice(SHARED, CB)), (wup, wup_h, wup_l, slice(SHARED, CB)),
                                      (wgate, wgate_h, wgate_l, slice(0, SHARED)), (wup, wup_h, wup_l, slice(0, SHARED)))[i]
                dve.wait_ge(act_wh, i + 1)
                dve.tensor_tensor(low[:, b], full[:, b], high[:, b].bitcast(F32), ALU.subtract).then_inc(dve_w, 1)

            def route(j):
                if j >= 1:
                    dve.wait_ge(act_re, j)
                dve.wait_ge(pe_log, j + 1)
                L = b_rt[j][:, 0:GROUPS * E].rearrange("p (g e) -> p g e", e=E)

                def wide(v):
                    return v.unsqueeze(2).broadcast_to([P, GROUPS, E])

                for g in range(GROUPS):
                    ins = dve.max(top[:, g], L[:, g])
                link(ins)
                dve.tensor_tensor(rt[:, 0], L, wide(top[:, :, 0]), ALU.subtract).then_inc(dve_ld, 1)
                for g in range(GROUPS):
                    ins = dve.max_index(topi[:, g], top[:, g], L[:, g])
                link(ins)
                ex = expert[:].unsqueeze(1).broadcast_to([P, GROUPS, E])
                for t in range(2):
                    ins = dve.tensor_tensor(rt[:, 1 + t], ex, wide(topi[:, :, t]), ALU.is_equal)
                link(ins)
                link(dve.tensor_tensor(rt[:, 3], rt[:, 1], rt[:, 2], ALU.add))
                dve.wait_ge(act_re, j + 1)
                dve.tensor_tensor(rt[:, 4], expo[:], rt[:, 3], ALU.mult)
                link(dve.tensor_reduce(rs[:, 0], expo[:], AX_X, ALU.add))
                if j < HALVES:
                    link(dve.tensor_reduce(rs[:, 1], rt[:, 4], AX_X, ALU.add))
                    link(dve.scalar_tensor_tensor(rs[:, 2], rs[:, 0], 1e-20, rs[:, 1], ALU.mult, ALU.add))
                    link(dve.reciprocal(rs[:, 3], rs[:, 2]))
                else:
                    link(dve.reciprocal(rs[:, 3], rs[:, 0]))
                link(dve.tensor_tensor(rt[:, 4], rt[:, 4], wide(rs[:, 3]), ALU.mult))
                if j >= 1:
                    dve.wait_ge(pe_gT, j)
                link(dve.tensor_copy(wsplit[:, :, 0:E], rt[:, 4]))
                dve.tensor_tensor(wsplit[:, :, E:2 * E], rt[:, 4], wsplit[:, :, 0:E].bitcast(F32),
                                  ALU.subtract).then_inc(dve_split, 1)

            def gate_up(c, n):
                k = CB * c + n
                dve.wait_ge(act_g, k + 1)
                g = gate_s[:, k % 2]
                link(dve.scalar_tensor_tensor(leaky[:, k % 2], g, LEAK, g, ALU.mult, ALU.max))
                dve.wait_ge(pe_u, k + 1)
                if c and n < 2:
                    dve.wait_ge(pool_mid, ROUTED * c)
                    dve.wait_ge(pe_down, CB * c)
                elif n == 2:
                    dve.wait_ge(pe_down, CB * c + 1)
                elif n > 2:
                    dve.wait_ge(pool_mid, ROUTED * c + n - 2)
                dve.tensor_tensor(gu[:, n % 2], leaky[:, k % 2], b_h1[:], ALU.mult).then_inc(dve_gu, 1)

            def norm(j):
                slot, c = j // HALVES, j % HALVES
                src = (y_tok, x1_tok)[slot][:, c]
                if slot == 0:
                    dve.wait_ge(act_y, c + 1)
                for g in range(GROUPS):
                    ins = dve.bn_stats(stat6[:, g], src[:, g])
                link(ins)
                for g in range(GROUPS):
                    ins = dve.bn_aggr(stat2[:, g], stat6[:, g])
                link(ins)
                v, y, t = (lnw[:, i] for i in range(3))
                link(dve.tensor_scalar(v, stat2[:, :, 1], EPS, None, ALU.add))
                link(dve.tensor_scalar(t.bitcast(I32), v.bitcast(I32), 1, None, ALU.arith_shift_right))
                link(dve.tensor_scalar(y.bitcast(I32), t.bitcast(I32), -1.0, float(RSQRT_SEED), ALU.mult, ALU.add))
                for _step in range(3):
                    link(dve.tensor_tensor(t, y, y, ALU.mult))
                    link(dve.scalar_tensor_tensor(t, t, -0.5, v, ALU.mult, ALU.mult))
                    link(dve.scalar_tensor_tensor(y, t, 1.5, y, ALU.add, ALU.mult))
                if c:
                    dve.wait_ge(pe_hT, j)
                for g in range(GROUPS):
                    ins = dve.tensor_scalar(hn[:, slot, g], src[:, g], stat2[:, g, 0:1], y[:, g:g + 1],
                                            ALU.subtract, ALU.mult)
                ins.then_inc(dve_hn, 1)
                dve.wait_ge(dve_hn, j + 1)

            def norm_split(j):
                high, low = ((hT_h[:], hT_l[:]), (hT_h[:], hT_l[:]),
                             (h2_h[:, 0], h2_l[:, 0]), (h2_h[:, 1], h2_l[:, 1]))[j]
                dve.wait_ge(act_hT, j + 1)
                if j == 1:
                    dve.wait_ge(pe_k, 1)
                dve.tensor_copy(high, hT[:, j // HALVES]).then_inc(dve_hh, 1)
                dve.wait_ge(dve_hh, j + 1)
                dve.tensor_tensor(low, hT[:, j // HALVES], high.bitcast(F32), ALU.subtract).then_inc(dve_hl, 1)

            def soft_max(c, r):
                dve.wait_ge(pe_s, RT * c + r + 1)
                s = b_s[r % 2][:].rearrange("p (q t) -> p q t", t=SEQ)
                link(dve.tensor_reduce(mx[:, r], s, AX_X, ALU.max))
                if c:
                    dve.wait_ge(pe_pT, RT * (c - 1) + r + 1)
                dve.tensor_tensor(prob[:, r].rearrange("p (q t) -> p q t", t=SEQ), s,
                                  mx[:, r].unsqueeze(2).broadcast_to([P, GROUPS * HG, SEQ]),
                                  ALU.subtract).then_inc(dve_dif, 1)

            def soft_sum(c, r):
                dve.wait_ge(act_exp, RT * c + r + 1)
                dve.tensor_reduce(psum[:, :, r], prob[:, r].rearrange("p (g h t) -> p g h t", g=GROUPS, h=HG),
                                  AX_X, ALU.add).then_inc(dve_sum, 1)

            def attend(c):
                dve.wait_ge(dve_sum, RT * (c + 1))
                link(dve.reciprocal(rsum[:], psum[:].rearrange("p g r h -> p (g r h)")))
                dve.wait_ge(pe_pv, RT * (c + 1))
                if c:
                    dve.wait_ge(pe_aT, c)
                dve.tensor_tensor(att.rearrange("p g (n d) -> p (g n) d", d=HD),
                                  b_o[:].rearrange("p (q d) -> p q d", d=HD),
                                  rsum[:].unsqueeze(2).broadcast_to([P, GROUPS * HEADS, HD]),
                                  ALU.mult).then_inc(dve_att, 1)

            def residual(c):
                dve.wait_ge(pe_o, c + 1)
                dve.wait_ge(pool_yb, c + 1)
                dve.tensor_tensor(x1_tok[:, c], b_s1[:].rearrange("p (g h) -> p g h", h=D), y_tok[:, c],
                                  ALU.add).then_inc(dve_x1, 1)
                dve.wait_ge(dve_x1, c + 1)

            def ffn(c, i):
                k = FB * c + i
                dve.wait_ge(act_gel, k + 1)
                if i % 2 == 0:
                    dve.wait_ge(pe_wb, ROUTED * HALVES + E * c + i // 2 + 1)
                if k >= 2:
                    dve.wait_ge(pool_lo, k - 1)
                dve.tensor_tensor(pm[:, k % 2], gel[:, k % 2], b_we[c][i // 2 % len(b_we[c])][:],
                                  ALU.mult).then_inc(dve_pm, 1)
                dve.wait_ge(dve_pm, k + 1)
                if k >= LAG:
                    dve.wait_ge(pe_y, k - LAG + 1)
                dve.tensor_copy(p_h[:, k % LAG], pm[:, k % 2]).then_inc(dve_ph, 1)

            def finish(c):
                dve.wait_ge(pe_yT, c + 1)
                dve.wait_ge(pool_xo, c + 1)
                dve.tensor_tensor(o_tok[:, c], b_o[:].rearrange("p (g h) -> p g h", h=D), x_tok[:, c],
                                  ALU.add).then_inc(dve_out, 1)

            for e in range(E):
                dve.memset(expert[:, e:e + 1], float(e)).then_inc(dve_const, 1)
            w_low(0)
            w_low(1)
            x_split(0)
            w_low(2)
            w_low(3)
            dve.wait_ge(pool_const, 3)
            for dst, src in ((sel_r, sel), (causal_r, causal[:])):
                dve.tensor_copy(dst[:], src).then_inc(dve_const, 1)
            dve.tensor_copy(ident_r[:], ident[0:SEQ, 0:SEQ].unsqueeze(1).broadcast_to([SEQ, GB, SEQ])
                            ).then_inc(dve_const, 1)
            dve.tensor_copy(selp_r[:].rearrange("k j (u m) -> k (j u) m", m=M), sel[:, :, 0:M]).then_inc(dve_const, 1)
            dve.tensor_reduce(headmask[:], head16[:].rearrange("p a h -> p h a"), AX_X, ALU.add).then_inc(dve_const, 1)
            dve.wait_ge(dve_const, E + 5)
            gate_up(0, 0)
            route(0)
            gate_up(0, 1)
            x_split(1)
            gate_up(0, 2)
            dve.wait_ge(act_proj, 1)
            dve.tensor_copy(qkT_h[:], projT[:, 0:2]).then_inc(dve_qk, 1)
            dve.wait_ge(dve_qk, 1)
            dve.tensor_tensor(qkT_l[:], projT[:, 0:2], qkT_h[:].bitcast(F32), ALU.subtract).then_inc(dve_qk, 1)
            dve.wait_ge(act_cols, 3)
            dve.tensor_scalar(bias_k[:], headmask[:], cols[:, ROW_BK:ROW_BK + 1], None, ALU.mult).then_inc(dve_qk, 1)
            gate_up(0, 3)
            gate_up(0, 4)
            norm(0)
            gate_up(1, 0)
            norm_split(0)
            route(1)
            gate_up(1, 1)
            gate_up(1, 2)
            for r in range(RT):
                soft_max(0, r)
                if r < 2:
                    gate_up(1, 3 + r)
                if r >= 1:
                    soft_sum(0, r - 1)
            norm(1)
            soft_sum(0, 3)
            attend(0)
            norm_split(1)
            residual(0)
            norm(2)
            norm_split(2)
            soft_max(1, 0)
            route(2)
            for r in range(1, RT):
                soft_max(1, r)
            for i in range(FB):
                ffn(0, i)
                if 1 <= i < 5:
                    soft_sum(1, i - 1)
                if i == 5:
                    attend(1)
                if i == 8:
                    residual(1)
                    norm(3)
                if i == 12:
                    norm_split(3)
            route(3)
            for i in range(FB):
                ffn(1, i)
                if i == 1:
                    finish(0)
            finish(1)

        @block.tensor
        def _(pe):
            def three(dst, wh, wl, xh, xl, first, last, before_low=None):
                pe.matmul(dst, wh, xh, start=first, stop=False)
                pe.matmul(dst, wl, xh, start=False, stop=False)
                if before_low:
                    pe.wait_ge(*before_low)
                return pe.matmul(dst, wh, xl, start=False, stop=last)

            def x_T(c):
                pe.wait_ge(ld_x[c], 16 * GB)
                for g in range(GROUPS):
                    ins = pe.transpose(b_s[c][:, g * P:(g + 1) * P], x_tok[:, c, g], ident[:])
                ins.then_inc(pe_x, 1)

            def block_up(c, n):
                k, j = CB * c + n, ORDER[n]
                if k < 2:
                    pe.wait_ge(dve_w, 2 * k + 2)
                if n == 0:
                    pe.wait_ge(dve_xh, c + 1)
                if k >= 1:
                    pe.wait_ge(act_g, k)
                three(b_h0[:], wgate_h[:, j], wgate_l[:, j], xT_h[:, c], xT_l[:, c], True, True,
                      (dve_x, c + 1) if n == 0 else None).then_inc(pe_g, 1)
                if k >= 1:
                    pe.wait_ge(dve_gu, k)
                three(b_h1[:], wup_h[:, j], wup_l[:, j], xT_h[:, c], xT_l[:, c], True, True).then_inc(pe_u, 1)

            def weights_up(c, n):
                k, j = ROUTED * c + n, ORDER[n + 1]
                if n == 0:
                    pe.wait_ge(act_gT, c + 1)
                else:
                    pe.wait_ge(act_wb, k)
                pe.matmul(b_w[:], selp_r[:, j], gT[:, 0], start=True, stop=True).then_inc(pe_wb, 1)

            def block_down(c, n):
                j = ORDER[n]
                if n == 0:
                    pe.wait_ge(dve_gu, CB * c + 1)
                    if c == 0:
                        pe.wait_ge(ld_down, 32)
                    else:
                        pe.wait_ge(act_y, c)
                else:
                    pe.wait_ge(pool_mid, ROUTED * c + n)
                src = gu[:, 0] if n == 0 else mid[:, (n - 1) % 2]
                for g in range(GROUPS):
                    ins = pe.matmul(b_y[:, g * D:(g + 1) * D], src[:, g * P:(g + 1) * P], wdown[:, j],
                                    start=(n == 0 and g == 0), stop=(n == CB - 1), skip_group_check=True)
                ins.then_inc(pe_down, 1)

            def cond_logits(c):
                if c == 0:
                    pe.wait_ge(act_cols, 3)
                else:
                    pe.wait_ge(act_wb, ROUTED * c)
                pe.wait_ge(act_x, c + 1)
                for g in range(GROUPS):
                    dst = b_w[:, g * E:(g + 1) * E]
                    pe.matmul(dst, xT[:, c, g * P:(g + 1) * P], cols[:, ROW_WT:ROW_WT + E], start=True, stop=False)
                    ins = pe.matmul(dst, cond4[:].rearrange("k b s -> k (b s)"), gcols[:, GROW_WG:GROWS],
                                    start=False, stop=True)
                ins.then_inc(pe_log, 1)

            def route_T(j):
                pe.wait_ge(dve_split, j + 1)
                for g in range(GROUPS):
                    ins = pe.transpose(b_rt[j][0:2 * E, g * P:(g + 1) * P], wsplit[:, g].bitcast(F32), ident[:])
                ins.then_inc(pe_gT, 1)

            def norm_T(j):
                pe.wait_ge(dve_hn, j + 1)
                pe.wait_ge(*((act_cols, 3), (act_pT, RT), (act_hT, 2), (act_pT, 2 * RT))[j])
                for g in range(GROUPS):
                    ins = pe.transpose(b_t[:, g * P:(g + 1) * P], hn[:, j // HALVES, g], ident[:])
                ins.then_inc(pe_hT, 1)

            def qk(c):
                pe.wait_ge(dve_qk, 2)
                pe.wait_ge(dve_hh, c + 1)
                pe.wait_ge(*((act_x, 2), (act_aT, 1))[c])
                three(b_s0[:], qkT_h[:, 0], qkT_l[:, 0], hT_h[:], hT_l[:], True, True,
                      (dve_hl, c + 1)).then_inc(pe_q, 1)
                if c:
                    pe.wait_ge(dve_x1, c)
                three(b_s1[:], qkT_h[:, 1], qkT_l[:, 1], hT_h[:], hT_l[:], True, True).then_inc(pe_k, 1)

            def values_up(c):
                pe.wait_ge(act_hT, (1, 3)[c])
                wv = projT[:, 2].rearrange("p (r h d) -> p h r d", r=RT, h=HG)
                for b in range(NB):
                    for h in range(HG):
                        ins = pe.matmul(b_t[h * SEQ:(h + 1) * SEQ, b * RT * HD:(b + 1) * RT * HD],
                                        hT[:, 0, b * SEQ:(b + 1) * SEQ], wv[:, h], start=True, stop=True)
                ins.then_inc(pe_v, 1)

            def scores(c, r):
                if r == 0:
                    pe.wait_ge(act_qk, c + 1)
                elif r >= 2:
                    pe.wait_ge(dve_dif, RT * c + r - 1)
                dst = b_s[r % 2]
                pe.matmul(dst[:], ident_r[:].rearrange("k b s -> k (b s)"),
                          causal_r[:].unsqueeze(1).broadcast_to([SEQ, GROUPS * HG, SEQ]),
                          start=True, stop=False, skip_group_check=True)
                ch = slice(r * HG * HD, (r + 1) * HG * HD)
                for g in range(GROUPS):
                    for b in range(GB):
                        col = (g * GB + b) * SEQ
                        ins = pe.matmul(dst[b * SEQ:(b + 1) * SEQ, g * HG * SEQ:(g + 1) * HG * SEQ],
                                        qT[ch, col:col + SEQ], kx[ch, :, col:col + SEQ],
                                        start=False, stop=True, skip_group_check=True)
                ins.then_inc(pe_s, 1)

            def prob_T(c, r):
                pe.wait_ge(act_exp, RT * c + r + 1)
                if r == 0:
                    pe.wait_ge(act_v, c + 1)
                else:
                    pe.wait_ge(act_pT, RT * c + r)
                for g in range(GROUPS):
                    ins = pe.transpose(b_t[:, g * P:(g + 1) * P], prob[:, r, g * P:(g + 1) * P], ident[:])
                ins.then_inc(pe_pT, 1)

            def values(c, r):
                pe.wait_ge(act_pT, RT * c + r + 1)
                if r == 0:
                    pe.wait_ge(pool_vx, c + 1)
                    pe.wait_ge(*((act_proj, 1), (dve_att, 1))[c])
                w = HG * HD
                for g in range(GROUPS):
                    for b in range(GB):
                        q = g * GB + b
                        ins = pe.matmul(b_o[b * SEQ:(b + 1) * SEQ, g * D + r * w:g * D + (r + 1) * w],
                                        probT[:, r, q * SEQ:(q + 1) * SEQ], vx[:, q, r], start=True, stop=True)
                ins.then_inc(pe_pv, 1)

            def att_T(c):
                pe.wait_ge(dve_att, c + 1)
                for g in range(GROUPS):
                    ins = pe.transpose(b_s0[:, g * P:(g + 1) * P], att[:, g], ident[:])
                ins.then_inc(pe_aT, 1)

            def project(c):
                pe.wait_ge(act_aT, c + 1)
                for g in range(GROUPS):
                    ins = pe.matmul(b_s1[:, g * D:(g + 1) * D], attT[:, g * P:(g + 1) * P], projT[:, 3],
                                    start=True, stop=True)
                ins.then_inc(pe_o, 1)

            def ffn_logits(c):
                pe.wait_ge(act_hT, c + 3)
                pe.wait_ge(*((act_wb, ROUTED * HALVES), (act_aT, HALVES))[c])
                for g in range(GROUPS):
                    ins = pe.matmul(b_rt[HALVES + c][:, g * E:(g + 1) * E], hT[:, 1, g * P:(g + 1) * P],
                                    cols[:, ROW_ROUTER:ROW_ROUTER + E], start=True, stop=True)
                ins.then_inc(pe_log, 1)

            def ffn_up(c, i):
                k = FB * c + i
                banks = b_h[c]
                if c == 0:
                    if i % 4 == 0:
                        pe.wait_ge(pool_w1, i // 4 + 1)
                if i == 0:
                    pe.wait_ge(dve_hh, c + 3)
                    if c == 0:
                        pe.wait_ge(act_g, CB * HALVES)
                        pe.wait_ge(dve_gu, CB * HALVES)
                if c and i < len(banks):
                    pe.wait_ge(*((act_gel, FB - 1), (act_gel, FB), (act_gT, 4), (dve_x1, HALVES))[i])
                elif i >= len(banks):
                    pe.wait_ge(act_gel, k - len(banks) + 1)
                three(banks[i % len(banks)][:], w1_h[:, i], w1_l[:, i], h2_h[:, c], h2_l[:, c], True, True,
                      (dve_hl, c + 3) if i == 0 else None).then_inc(pe_h, 1)

            def ffn_weights(c, e):
                banks = b_we[c]
                if e == 0:
                    pe.wait_ge(act_gT, HALVES + c + 1)
                if c and e < len(banks):
                    pe.wait_ge(*((dve_pm, FB), (act_hT, 4))[e])
                elif e >= len(banks):
                    pe.wait_ge(dve_pm, FB * c + 2 * (e - len(banks)) + 2)
                pe.matmul(banks[e % len(banks)][:], sel_r[:, e], gT[:, GT_SLOT[HALVES + c]], start=True,
                          stop=True).then_inc(pe_wb, 1)

            def ffn_down(c, i):
                k = FB * c + i
                pe.wait_ge(dve_ph, k + 1)
                if c == 0 and i % 4 == 0:
                    pe.wait_ge(pool_w2, i // 4 + 1)
                if i == 0:
                    pe.wait_ge(*((act_y, HALVES) if c == 0 else (act_yT, c)))
                three(b_y[:], w2_h[:, i], w2_l[:, i], p_h[:, k % LAG], p_l[:, k % LAG], i == 0, i == FB - 1,
                      (pool_lo, k + 1)).then_inc(pe_y, 1)

            def y_T(c):
                pe.wait_ge(act_yT, c + 1)
                pe.wait_ge(dve_att, HALVES)
                if c:
                    pe.wait_ge(dve_out, c)
                for g in range(GROUPS):
                    ins = pe.transpose(b_o[:, g * P:(g + 1) * P], yT[:, g * P:(g + 1) * P], ident[:])
                ins.then_inc(pe_yT, 1)

            pe.wait_ge(pool_const, 1)
            x_T(0)
            block_up(0, 0)
            pe.wait_ge(ld_rows, 7 * 16)
            pe.wait_ge(ld_cond, 2 * 16)
            pe.wait_ge(pool_const, 2)
            pe.transpose(b_t[:, 0:ROWS], rows[:], ident[0:ROWS, 0:ROWS])
            pe.transpose(b_t[:, ROWS:ROWS + GROWS], grows[:], ident[0:GROWS, 0:GROWS]).then_inc(pe_cols, 1)
            block_up(0, 1)
            cond_logits(0)
            block_down(0, 0)
            x_T(1)
            pe.wait_ge(ld_proj, 3 * 16)
            for k in range(4):
                ins = pe.transpose(b_o[:, k * P:(k + 1) * P], proj[:, k], ident[:])
            ins.then_inc(pe_proj, 1)
            block_up(0, 2)
            route_T(0)
            weights_up(0, 0)
            block_up(0, 3)
            block_down(0, 1)
            weights_up(0, 1)
            block_up(0, 4)
            block_down(0, 2)
            weights_up(0, 2)
            block_down(0, 3)
            weights_up(0, 3)
            block_up(1, 0)
            block_down(0, 4)
            cond_logits(1)
            block_up(1, 1)
            norm_T(0)
            block_down(1, 0)
            qk(0)
            values_up(0)
            route_T(1)
            weights_up(1, 0)
            block_up(1, 2)
            scores(0, 0)
            scores(0, 1)
            block_down(1, 1)
            weights_up(1, 1)
            for r in range(RT):
                prob_T(0, r)
                if r < 2:
                    block_up(1, r + 3)
                    scores(0, r + 2)
                if r < 3:
                    block_down(1, r + 2)
                if r < 2:
                    weights_up(1, r + 2)
                values(0, r)
            norm_T(1)
            att_T(0)
            project(0)
            qk(1)
            norm_T(2)
            ffn_logits(0)
            ffn_up(0, 0)
            ffn_up(0, 1)
            values_up(1)
            scores(1, 0)
            scores(1, 1)
            route_T(2)
            ffn_weights(0, 0)
            scores(1, 2)
            scores(1, 3)
            for i in range(2, FB + LAG):
                if i < FB:
                    ffn_up(0, i)
                    if i % 2 == 0:
                        ffn_weights(0, i // 2)
                if i >= LAG:
                    ffn_down(0, i - LAG)
                if 2 <= i < 6:
                    prob_T(1, i - 2)
                if 3 <= i < 7:
                    values(1, i - 3)
                if i == 8:
                    att_T(1)
                if i == 9:
                    project(1)
                if i == 13:
                    norm_T(3)
                if i == 15:
                    ffn_logits(1)
                if i == FB:
                    ffn_up(1, 0)
                if i == FB + 1:
                    ffn_up(1, 1)
            route_T(3)
            ffn_weights(1, 0)
            ffn_weights(1, 1)
            y_T(0)
            for i in range(2, FB + LAG):
                if i < FB:
                    ffn_up(1, i)
                    if i % 2 == 0 and i >= 4:
                        ffn_weights(1, i // 2)
                if i >= LAG:
                    ffn_down(1, i - LAG)
            y_T(1)


_INS = ['x', 'cond_64', 'L0_cond_wt', 'L0_cond_wg', 'L0_cond_w_gate', 'L0_cond_w_up', 'L0_cond_w_down',
        'L0_cond_sw_gate', 'L0_cond_sw_up', 'L0_cond_sw_down', 'L0_ffn_ln1_w', 'L0_ffn_ln1_b',
        'L0_ffn_in_proj_w', 'L0_ffn_in_proj_b', 'L0_ffn_out_proj_w', 'L0_ffn_out_proj_b', 'L0_ffn_ln2_w',
        'L0_ffn_ln2_b', 'L0_ffn_router_w', 'L0_ffn_w1', 'L0_ffn_w2']


def kernel(**inputs):
    import numpy as _np
    import concourse.bacc as _bacc
    from concourse import mybir as _mybir
    from concourse.bass_utils import run_bass_kernel_spmd as _run

    nc = _bacc.Bacc("TRN2", target_bir_lowering=False, num_devices=1)
    arrays, args = {}, []
    for name in _INS:
        a = _np.ascontiguousarray(inputs[name])
        arrays[f"in_{name}"] = a
        args.append(nc.dram_tensor(f"in_{name}", a.shape, _mybir.dt.from_np(a.dtype), kind="ExternalInput").ap())
    shape = inputs['x'].shape
    args.append(nc.dram_tensor("out_0", shape, _mybir.dt.float32, kind="ExternalOutput").ap())
    build(nc, *args)
    r = _run(nc, [arrays], core_ids=[0])
    return r.results[0]["out_0"]
```

```python
from contextlib import ExitStack

import concourse.bass as bass
from concourse import mybir

F32 = mybir.dt.float32
F32R = mybir.dt.float32r
I32 = mybir.dt.int32
U32 = mybir.dt.uint32
ALU = mybir.AluOpType
ACT = mybir.ActivationFunctionType
AX_X = mybir.AxisListType.X

P = 128
HALVES = 2
BATCH = 32
SEQ = 32
D = 128
GROUPS = 4
GB = 4
N = GROUPS * P
NB = GROUPS * GB
E = 8
M = 64
CB = E * M // P + 1
ROUTED = CB - 1
SHARED = CB - 1
F = 256
FB = E * F // P
LAG = 5
SLOTS = 4
LOW_TURN = 3
HEADS = 16
HD = D // HEADS
HG = 4
RT = HEADS // HG
EPS = 1e-5
LEAK = 0.01
MASKED = -1e30
RSQRT_SEED = 0x5F3759DF
HALLEY = 3 / 8

ROW_BQ, ROW_BK, ROW_BV, ROW_LN1W, ROW_LN1B, ROW_LN2W, ROW_LN2B = range(7)
ROW_WT, ROW_ROUTER, ROWS = 7, 15, 23
GROW_WG, GROWS = 32, 40


def build(nc, x, cond, wt, wg, w_gate, w_up, w_down, sw_gate, sw_up, sw_down, ln1_w, ln1_b, in_w, in_b,
          out_w, out_b, ln2_w, ln2_b, router_w, w1, w2, out):
    with ExitStack() as ctx:
        def sb(name, shape, dt=F32):
            return ctx.enter_context(nc.sbuf_tensor(name, shape, dt))

        def bank(name):
            return ctx.enter_context(nc.psum_tensor(name, [P, N], F32))

        def sem(name):
            return ctx.enter_context(nc.semaphore(name))

        b_h0 = bank("b_h0")
        b_h1 = bank("b_h1")
        b_w = bank("b_w")
        b_y = bank("b_y")
        b_s0 = bank("b_s0")
        b_s1 = bank("b_s1")
        b_t = bank("b_t")
        b_o = bank("b_o")
        b_s = [[b_s0, b_s1], [b_h0, b_h1]]
        b_tr = [b_t, b_w]
        b_ov = [b_o, b_y]
        b_h = ([b_s0, b_s1] * 2 + [b_s0, b_h1, b_s1] * 4,
               [b_s0, b_h1, b_s1, b_h0] * 4)
        b_we = [[b_t, b_h0], [b_w, b_t]]
        b_fin = [b_s0, b_s1, b_h1, b_h0]
        b_rt = [b_w, b_o, b_t, b_w]

        x_tok = sb("x_tok", [P, HALVES, GROUPS, D])
        rows = sb("rows", [ROWS, D])
        grows = sb("grows", [GROWS, D])
        cols = sb("cols", [P, ROWS])
        gcols = sb("gcols", [P, GROWS])
        cond4 = sb("cond4", [P, GB, SEQ])
        wgate = sb("wgate", [P, CB, P])
        wup = sb("wup", [P, CB, P])
        wdown = sb("wdown", [P, CB, D])
        wgate_h, wgate_l = sb("wgate_h", [P, CB, P], F32R), sb("wgate_l", [P, CB, P], F32R)
        wup_h, wup_l = sb("wup_h", [P, CB, P], F32R), sb("wup_l", [P, CB, P], F32R)
        proj = sb("proj", [P, 4, D])
        projT = sb("projT", [P, 4, D])
        qkT_h, qkT_l = sb("qkT_h", [P, 2, D], F32R), sb("qkT_l", [P, 2, D], F32R)
        bo = sb("bo", [P, D])
        w1_s = sb("w1_s", [P, FB, P])
        w2_s = sb("w2_s", [P, FB, D])
        w1_h, w1_l = sb("w1_h", [P, FB, P], F32R), sb("w1_l", [P, FB, P], F32R)
        w2_h, w2_l = sb("w2_h", [P, FB, D], F32R), sb("w2_l", [P, FB, D], F32R)

        ident = sb("ident", [P, P])
        ident_r = sb("ident_r", [SEQ, GB, SEQ], F32R)
        causal = sb("causal", [SEQ, SEQ])
        causal_r = sb("causal_r", [SEQ, SEQ], F32R)
        head16 = sb("head16", [P, RT, HG])
        headmask = sb("headmask", [P, HG])
        vmask = sb("vmask", [P, HG, HD])
        sel_r = sb("sel_r", [2 * E, E, P], F32R)
        selp_r = sb("selp_r", [2 * E, ROUTED, P], F32R)
        expert = sb("expert", [P, E])

        xT = sb("xT", [P, HALVES, N])
        xT_h, xT_l = sb("xT_h", [P, HALVES, N], F32R), sb("xT_l", [P, HALVES, N], F32R)
        kT = xT[:, 0]
        gate_s = sb("gate_s", [P, 2, N])
        leaky = sb("leaky", [P, 2, N])
        gu = sb("gu", [P, 2, N])
        mid = sb("mid", [P, 2, N])
        y_tok = sb("y_tok", [P, HALVES, GROUPS, D])
        hn = sb("hn", [P, 2, GROUPS, D])
        hT = sb("hT", [P, 2, N])
        hT_h, hT_l = sb("hT_h", [P, N], F32R), sb("hT_l", [P, N], F32R)
        h2_h, h2_l = sb("h2_h", [P, HALVES, N], F32R), sb("h2_l", [P, HALVES, N], F32R)
        qT = sb("qT", [P, N])
        kx = sb("kx", [P, HG, N])
        vc = sb("vc", [P, NB, RT, HD])
        vx = sb("vx", [P, NB, RT, HG, HD])
        mx = sb("mx", [P, RT, GROUPS * HG])
        prob = sb("prob", [P, RT, N])
        sel = prob[0:2 * E, 0:2].rearrange("k r (e p) -> k (r e) p", p=P)
        probT = sb("probT", [P, RT, N])
        psum = sb("psum", [P, GROUPS, RT, HG])
        fold = sb("fold", [P, GROUPS * HG, SEQ // 2])
        rsum = sb("rsum", [P, GROUPS * HEADS])
        att = wup[:, 0:GROUPS]
        attT = wgate[:, 0:GROUPS].rearrange("p g q -> p (g q)")
        x1_tok = sb("x1_tok", [P, HALVES, GROUPS, D])
        p_h, p_l = sb("p_h", [P, LAG, N], F32R), sb("p_l", [P, LAG, N], F32R)
        gel = [buf[:, s] for buf in (gate_s, leaky) for s in range(2)]
        pm = w1_s[:].rearrange("p (s b) q -> p s (b q)", s=SLOTS)
        yT = w2_s[:, 0:GROUPS].rearrange("p b q -> p (b q)")
        o_tok = w2_s[:, GROUPS:3 * GROUPS].rearrange("p (c g) h -> p c g h", c=HALVES)
        stat6 = sb("stat6", [P, GROUPS, 6])
        stat2 = sb("stat2", [P, GROUPS, 2])
        lnw = sb("lnw", [P, 4, GROUPS])
        top = sb("top", [P, GROUPS, E])
        topi = sb("topi", [P, GROUPS, E], U32)
        rt = sb("rt", [P, 5, GROUPS, E])
        rs = sb("rs", [P, 4, GROUPS])
        expo = sb("expo", [P, GROUPS, E])
        wsplit = sb("wsplit", [P, GROUPS, 2 * E], F32R)
        logit_g = sb("logit_g", [P, E])
        logit = sb("logit", [P, GROUPS, E])
        gT = sb("gT", [2 * E, 2, N], F32R)

        ld_x = [sem("ld_x0"), sem("ld_x1")]
        ld_rows, ld_cond, ld_shared, ld_gate, ld_up, ld_down, ld_proj, ld_w1, ld_w2 = (
            sem(s) for s in ("ld_rows", "ld_cond", "ld_shared", "ld_gate", "ld_up", "ld_down", "ld_proj",
                             "ld_w1", "ld_w2"))
        pool_const, pool_chain, pool_yb, pool_vx, pool_xo, pool_lo, pool_w1, pool_w2 = (
            sem(s) for s in ("pool_const", "pool_chain", "pool_yb", "pool_vx", "pool_xo",
                             "pool_lo", "pool_w1", "pool_w2"))
        act_cols, act_x, act_proj, act_g, act_gT, act_y, act_hT, act_qk, act_exp, act_pT = (
            sem(s) for s in ("act_cols", "act_x", "act_proj", "act_g", "act_gT", "act_y", "act_hT",
                             "act_qk", "act_exp", "act_pT"))
        act_aT, act_re, act_gel, act_yT, act_w1, act_w2, act_wh = (
            sem(s) for s in ("act_aT", "act_re", "act_gel", "act_yT", "act_w1", "act_w2", "act_wh"))
        dve_chain, dve_const, act_xh, dve_x, dve_w, dve_gu, dve_split, dve_ld, dve_hn = (
            sem(s) for s in ("dve_chain", "dve_const", "act_xh", "dve_x", "dve_w", "dve_gu", "dve_split",
                             "dve_ld", "dve_hn"))
        dve_hl, dve_kx, dve_dif, dve_att, dve_x1, dve_pm, dve_lo, dve_out, dve_qk = (
            sem(s) for s in ("dve_hl", "dve_kx", "dve_dif", "dve_att", "dve_x1", "dve_pm", "dve_lo",
                             "dve_out", "dve_qk"))
        pe_x, pe_cols, pe_proj, pe_g, pe_u, pe_wb, pe_down, pe_log, pe_gT, pe_hT = (
            sem(s) for s in ("pe_x", "pe_cols", "pe_proj", "pe_g", "pe_u", "pe_wb", "pe_down", "pe_log",
                             "pe_gT", "pe_hT"))
        pe_q, pe_k, pe_v, pe_s, pe_pT, pe_pv, pe_sum, pe_aT, pe_o, pe_h, pe_y, pe_yT = (
            sem(s) for s in ("pe_q", "pe_k", "pe_v", "pe_s", "pe_pT", "pe_pv", "pe_sum", "pe_aT", "pe_o",
                             "pe_h", "pe_y", "pe_yT"))
        act_k, act_hh, act_ph = sem("act_k"), sem("act_hh"), sem("act_ph")
        act_v, act_lg, act_hn, pool_sum, dve_sum, dve_mid, dve_rs, pe_lg = (
            sem(s) for s in ("act_v", "act_lg", "act_hn", "pool_sum", "dve_sum", "dve_mid", "dve_rs", "pe_lg"))
        st_out = sem("st_out")

        def low_on_vector(c, i):
            return i >= FB - 2 or (c == 1 and i % LOW_TURN == 0)

        def low_done(k):
            mine = sum(low_on_vector(i // FB, i % FB) for i in range(k + 1))
            return (dve_lo, mine) if low_on_vector(k // FB, k % FB) else (pool_lo, k + 1 - mine)

        GT_SLOT = [0, 0, 1, 0]
        ORDER = [SHARED, 0, 1, 2, 3]
        block = ctx.enter_context(nc.Block())

        def tile_rows(ap, c, b):
            return ap.rearrange("s (c g b) h -> c b s g h", c=HALVES, g=GROUPS)[c, b]

        def tile_out(g):
            return out.rearrange("s (c g b) h -> c g b s h", c=HALVES, g=GROUPS)[1, g]

        @block.sync
        def _(sp):
            for b in range(0, GB // 2):
                sp.dma_start(x_tok[b * SEQ:(b + 1) * SEQ, 0], tile_rows(x, 0, b)).then_inc(ld_x[0], 16)
            sp.dma_start(wgate[:, SHARED, :], sw_gate).then_inc(ld_shared, 16)
            sp.dma_start(wup[:, SHARED, :], sw_up).then_inc(ld_shared, 16)
            sp.dma_start(wgate[:, 0:SHARED, :].rearrange("h j (u m) -> h (j u) m", m=M),
                         w_gate.rearrange("e h m -> h e m")).then_inc(ld_gate, 16)
            sp.dma_start(wup[:, 0:SHARED, :].rearrange("h j (u m) -> h (j u) m", m=M),
                         w_up.rearrange("e h m -> h e m")).then_inc(ld_up, 16)
            for at, src in ((ROW_WT, wt), (ROW_BQ, in_b.rearrange("(k h) -> k h", k=3)), (ROW_LN1W, ln1_w.unsqueeze(0)),
                            (ROW_LN1B, ln1_b.unsqueeze(0)), (ROW_LN2W, ln2_w.unsqueeze(0)),
                            (ROW_LN2B, ln2_b.unsqueeze(0)), (ROW_ROUTER, router_w)):
                sp.dma_start(rows[at:at + src.shape[0], :], src).then_inc(ld_rows, 16)
            sp.dma_start(grows[0:GROW_WG, 0:M], cond).then_inc(ld_cond, 16)
            sp.dma_start(grows[GROW_WG:GROWS, 0:M], wg).then_inc(ld_cond, 16)
            sp.dma_start(wdown[:, 0:SHARED, :],
                         w_down.rearrange("e m h -> (e m) h").rearrange("(j p) h -> p j h", p=P)).then_inc(ld_down, 16)
            sp.dma_start(wdown[:, SHARED, :], sw_down).then_inc(ld_down, 16)
            for b in range(GB):
                sp.dma_start(x_tok[b * SEQ:(b + 1) * SEQ, 1], tile_rows(x, 1, b)).then_inc(ld_x[1], 16)
            sp.dma_start(proj[:, 0:3, :], in_w.rearrange("(k p) h -> p k h", p=P)).then_inc(ld_proj, 16)
            sp.dma_start(proj[:, 3, :], out_w).then_inc(ld_proj, 16)
            sp.dma_start(bo[:], out_b.partition_broadcast(P)).then_inc(ld_proj, 16)
            sp.dma_start(w1_s[:].rearrange("h (e b) p -> h e (b p)", e=E),
                         w1.rearrange("e h f -> h e f")).then_inc(ld_w1, 16)
            sp.dma_start(w2_s[:], w2.rearrange("e (b p) h -> p (e b) h", p=P)).then_inc(ld_w2, 16)
            sp.wait_ge(dve_out, 1)
            for b in range(GB):
                sp.dma_start(tile_rows(out, 0, b), o_tok[b * SEQ:(b + 1) * SEQ, 0]).then_inc(st_out, 16)
            for g in range(0, GROUPS, 2):
                sp.wait_ge(dve_out, g + 2)
                sp.dma_start(tile_out(g), o_tok[:, 1, g]).then_inc(st_out, 16)
            sp.wait_ge(st_out, 16 * (GB + GROUPS))

        @block.gpsimd
        def _(pool):
            chain = [0]

            def link(ins):
                chain[0] += 1
                ins.then_inc(pool_chain, 1)
                pool.wait_ge(pool_chain, chain[0])

            link(pool.memset(ident[:], 0.0))
            pool.affine_select(out=ident[:], in_=ident[:], compare_op=ALU.not_equal, fill=1.0, base=0,
                               pattern=[[-1, P]], channel_multiplier=1).then_inc(pool_const, 1)
            pool.memset(grows[:, M:D], 0.0).then_inc(pool_const, 1)
            link(pool.memset(sel, 0.0))
            for part in range(2):
                link(pool.affine_select(out=sel, in_=sel, compare_op=ALU.not_equal, fill=1.0, base=-E * part,
                                        pattern=[[-1, E], [0, P]], channel_multiplier=1))
            link(pool.memset(causal[:], 0.0))
            link(pool.affine_select(out=causal[:], in_=causal[:], compare_op=ALU.is_ge, fill=MASKED, base=0,
                                    pattern=[[-1, SEQ]], channel_multiplier=1))
            link(pool.memset(head16[:], 1.0))
            link(pool.affine_select(out=head16[:], in_=head16[:], compare_op=ALU.is_ge, fill=0.0, base=0,
                                    pattern=[[-SEQ, RT], [-HD, HG]], channel_multiplier=1))
            link(pool.affine_select(out=head16[:], in_=head16[:], compare_op=ALU.is_ge, fill=0.0, base=HD - 1,
                                    pattern=[[SEQ, RT], [HD, HG]], channel_multiplier=-1))
            link(pool.memset(vmask[:], 1.0))
            link(pool.affine_select(out=vmask[:], in_=vmask[:], compare_op=ALU.is_ge, fill=0.0, base=0,
                                    pattern=[[-SEQ, HG], [0, HD]], channel_multiplier=1))
            pool.affine_select(out=vmask[:], in_=vmask[:], compare_op=ALU.is_ge, fill=0.0, base=SEQ - 1,
                               pattern=[[SEQ, HG], [0, HD]], channel_multiplier=-1).then_inc(pool_const, 1)

            def residual_bias(c):
                pool.wait_ge(act_y, c + 1)
                if c == 0:
                    pool.wait_ge(ld_proj, 48)
                pool.wait_ge(act_hn, c + 1)
                pool.wait_ge(dve_hn, c + 1)
                pool.tensor_tensor(y_tok[:, c], y_tok[:, c], bo[:].unsqueeze(1).broadcast_to([P, GROUPS, D]),
                                   ALU.add).then_inc(pool_yb, 1)

            def spread_values(c, r):
                if r == 0:
                    pool.wait_ge(act_v, c + 1)
                if c:
                    pool.wait_ge(pe_pv, r + 1)
                pool.tensor_tensor(vx[:, :, r], vc[:, :, r].unsqueeze(2).broadcast_to([P, NB, HG, HD]),
                                   vmask[:].unsqueeze(1).broadcast_to([P, NB, HG, HD]),
                                   ALU.mult).then_inc(pool_vx, 1)

            def soft_sum(c, r):
                pool.wait_ge(act_exp, RT * c + r + 1)
                if c or r:
                    pool.wait_ge(pool_sum, (RT - 1) * c + r)
                if c and r == 0:
                    pool.wait_ge(dve_att, c)
                p, width = prob[:, r].rearrange("p (q t) -> p q t", t=SEQ), SEQ // 2
                link(pool.tensor_tensor(fold[:], p[:, :, 0:width], p[:, :, width:SEQ], ALU.add))
                while width > 2:
                    width //= 2
                    link(pool.tensor_tensor(fold[:, :, 0:width], fold[:, :, 0:width], fold[:, :, width:2 * width],
                                            ALU.add))
                f = fold[:].rearrange("p (g h) t -> p g h t", g=GROUPS)
                pool.tensor_tensor(psum[:, :, r], f[:, :, :, 0], f[:, :, :, 1], ALU.add).then_inc(pool_sum, 1)

            def residual_in(c):
                pool.wait_ge(dve_x1, c + 1)
                pool.tensor_tensor(x_tok[:, c], x_tok[:, c], x1_tok[:, c], ALU.add).then_inc(pool_xo, 1)

            def ffn_low(c, i):
                k = FB * c + i
                if low_on_vector(c, i):
                    return
                pool.wait_ge(act_ph, k + 1)
                if k >= LAG:
                    pool.wait_ge(pe_y, k - LAG + 1)
                pool.tensor_tensor(p_l[:, k % LAG], pm[:, k % SLOTS], p_h[:, k % LAG].bitcast(F32),
                                   ALU.subtract).then_inc(pool_lo, 1)

            def weight_low(which, i):
                full, high, low, src, dst = ((w1_s, w1_h, w1_l, act_w1, pool_w1), (w2_s, w2_h, w2_l, act_w2, pool_w2))[which]
                pool.wait_ge(src, i + 1)
                b = slice(4 * i, 4 * i + 4)
                pool.tensor_tensor(low[:, b], full[:, b], high[:, b].bitcast(F32), ALU.subtract).then_inc(dst, 1)

            for which in range(2):
                for n in range(FB // 4):
                    weight_low(which, n)
            for r in range(RT):
                spread_values(0, r)
            soft_sum(0, 0)
            residual_bias(0)
            soft_sum(0, 1)
            soft_sum(0, 2)
            spread_values(1, 0)
            spread_values(1, 1)
            spread_values(1, 2)
            spread_values(1, 3)
            for r in range(RT - 1):
                soft_sum(1, r)
            residual_bias(1)
            residual_in(0)
            for i in range(FB):
                ffn_low(0, i)
            residual_in(1)
            for i in range(FB):
                ffn_low(1, i)

        @block.scalar
        def _(act):
            for b in range(GB // 2, GB):
                act.dma_start(x_tok[b * SEQ:(b + 1) * SEQ, 0], tile_rows(x, 0, b)).then_inc(ld_x[0], 16)

            def x_in(c):
                act.wait_ge(pe_x, c + 1)
                nc.scalar.copy(xT_h[:, c], b_s[0][c][:]).then_inc(act_xh, 1)
                nc.scalar.copy(xT[:, c], b_s[0][c][:]).then_inc(act_x, 1)

            def gate_copy(c, n):
                k = CB * c + n
                act.wait_ge(pe_g, k + 1)
                if k >= 2:
                    act.wait_ge(dve_gu, k - 1)
                nc.scalar.copy(gate_s[:, k % 2], b_h0[:]).then_inc(act_g, 1)

            def norm_apply(j):
                slot, c = j // HALVES, j % HALVES
                act.wait_ge(dve_rs, j + 1)
                if c:
                    act.wait_ge(pe_hT, j)
                for g in range(GROUPS // 2):
                    ins = nc.scalar.activation(hn[:, slot, g], (y_tok, x1_tok)[slot][:, c, g], ACT.Identity,
                                               scale=lnw[:, 1, g:g + 1], bias=lnw[:, 3, g:g + 1])
                ins.then_inc(act_hn, 1)

            def route_exp(j, scale):
                act.wait_ge(dve_ld, j + 1)
                nc.scalar.activation(expo[:], rt[:, 0], ACT.Exp, scale=scale).then_inc(act_re, 1)

            def route_T(j):
                act.wait_ge(pe_gT, j + 1)
                nc.scalar.copy(gT[:, GT_SLOT[j]], b_rt[j][0:2 * E, :]).then_inc(act_gT, 1)

            def y_copy(c):
                act.wait_ge(pe_down, CB * (c + 1))
                nc.scalar.copy(y_tok[:, c].rearrange("p g h -> p (g h)"), b_y[:]).then_inc(act_y, 1)

            def norm_T(j):
                slot = j // HALVES
                w, b = ((ROW_LN1W, ROW_LN1B), (ROW_LN2W, ROW_LN2B))[slot]
                act.wait_ge(pe_hT, j + 1)
                if j == 1:
                    act.wait_ge(pe_k, 1)
                high = (hT_h[:], hT_h[:], h2_h[:, 0], h2_h[:, 1])[j]
                nc.scalar.activation(high, b_tr[j % HALVES][:], ACT.Identity, scale=cols[:, w:w + 1],
                                     bias=cols[:, b:b + 1]).then_inc(act_hh, 1)
                if j % HALVES:
                    act.wait_ge(dve_hl, j)
                    act.wait_ge(*((pe_v, 1) if slot == 0 else (pe_log, 3)))
                nc.scalar.activation(hT[:, slot], b_tr[j % HALVES][:], ACT.Identity, scale=cols[:, w:w + 1],
                                     bias=cols[:, b:b + 1]).then_inc(act_hT, 1)

            def q_copy(c):
                act.wait_ge(pe_q, c + 1)
                if c:
                    act.wait_ge(pe_s, RT * c)
                    act.wait_ge(dve_kx, c)
                nc.scalar.activation(qT[:], b_s[c][0][:], ACT.Identity, scale=1.0,
                                     bias=cols[:, ROW_BQ:ROW_BQ + 1])

            def k_copy(c):
                act.wait_ge(pe_k, c + 1)
                nc.scalar.activation(kT, b_s[c][1][:], ACT.Identity, scale=1.0,
                                     bias=cols[:, ROW_BK:ROW_BK + 1]).then_inc(act_k, 1)

            def k_spread(c):
                act.wait_ge(act_k, c + 1)
                for h in range(HG // 2):
                    ins = nc.scalar.mul(kx[:, h], kT, headmask[:, h:h + 1])
                ins.then_inc(act_qk, 1)

            def v_copy(c):
                act.wait_ge(pe_v, c + 1)
                if c:
                    act.wait_ge(pool_vx, RT * c)
                nc.scalar.copy(vc[:].rearrange("p b r d -> p (b r d)"), b_tr[c][:]).then_inc(act_v, 1)

            def soft_exp(c, r):
                act.wait_ge(dve_dif, RT * c + r + 1)
                nc.scalar.activation(prob[:, r], prob[:, r], ACT.Exp, scale=HD ** -0.5).then_inc(act_exp, 1)

            def prob_T(c, r):
                act.wait_ge(pe_pT, RT * c + r + 1)
                if c:
                    act.wait_ge(pe_pv, r + 1)
                nc.scalar.copy(probT[:, r], b_tr[c][:]).then_inc(act_pT, 1)

            def att_T(c):
                act.wait_ge(pe_aT, c + 1)
                if c:
                    act.wait_ge(pe_o, c)
                nc.scalar.activation(attT, b_s[c][0][:], ACT.Identity, scale=1.0,
                                     bias=cols[:, ROW_BV:ROW_BV + 1]).then_inc(act_aT, 1)

            def gelu(c, i):
                k = FB * c + i
                act.wait_ge(pe_h, k + 1)
                if k == 0:
                    act.wait_ge(dve_gu, HALVES * CB)
                if k >= SLOTS:
                    act.wait_ge(dve_pm, k - SLOTS + 1)
                nc.scalar.activation(gel[k % SLOTS], b_h[c][i][:], ACT.Gelu).then_inc(act_gel, 1)

            def ffn_high(c, i):
                k = FB * c + i
                act.wait_ge(dve_pm, k + 1)
                if k >= LAG:
                    act.wait_ge(pe_y, k - LAG + 1)
                nc.scalar.copy(p_h[:, k % LAG], pm[:, k % SLOTS]).then_inc(act_ph, 1)

            def y_out(c):
                act.wait_ge(pe_y, FB * (c + 1))
                if c == 0:
                    nc.scalar.copy(yT[:], b_o[:]).then_inc(act_yT, 1)
                    return
                act.wait_ge(pe_yT, 1)
                for g in range(GROUPS):
                    q = slice(P * g, P * (g + 1))
                    nc.scalar.copy(yT[:, q], b_y[:, q]).then_inc(act_yT, 1)
                for g in range(1, GROUPS, 2):
                    act.wait_ge(dve_out, g + 2)
                    act.dma_start(tile_out(g), o_tok[:, 1, g]).then_inc(st_out, 16)

            act.wait_ge(ld_shared, 32)
            for high, full in ((wgate_h, wgate), (wup_h, wup)):
                nc.scalar.copy(high[:, SHARED], full[:, SHARED]).then_inc(act_wh, 1)
            x_in(0)
            for high, full, ld in ((wgate_h, wgate, ld_gate), (wup_h, wup, ld_up)):
                act.wait_ge(ld, 16)
                nc.scalar.copy(high[:, 0:SHARED], full[:, 0:SHARED]).then_inc(act_wh, 1)
            gate_copy(0, 0)
            gate_copy(0, 1)
            act.wait_ge(pe_cols, 1)
            nc.scalar.copy(cols[:], b_t[:, 0:ROWS]).then_inc(act_cols, 1)
            nc.scalar.copy(gcols[:], b_t[:, ROWS:ROWS + GROWS]).then_inc(act_cols, 1)
            nc.scalar.copy(cond4[:], b_t[:, ROWS:ROWS + GROW_WG].unsqueeze(1).broadcast_to([P, GB, SEQ])
                           ).then_inc(act_cols, 1)
            def w_high(which, i):
                high, full, ld, done = ((w1_h, w1_s, ld_w1, act_w1), (w2_h, w2_s, ld_w2, act_w2))[which]
                if i == 0:
                    act.wait_ge(ld, 16)
                nc.scalar.copy(high[:, 4 * i:4 * i + 4], full[:, 4 * i:4 * i + 4]).then_inc(done, 1)

            act.wait_ge(pe_lg, 1)
            nc.scalar.copy(logit_g[:], b_t[:, 0:E]).then_inc(act_lg, 1)
            route_exp(0, 0.5)
            x_in(1)
            act.wait_ge(pe_proj, 1)
            nc.scalar.copy(projT[:].rearrange("p k h -> p (k h)"), b_o[:]).then_inc(act_proj, 1)
            gate_copy(0, 2)
            route_T(0)
            w_high(0, 0)
            w_high(0, 1)
            gate_copy(0, 3)
            w_high(0, 2)
            w_high(0, 3)
            gate_copy(0, 4)
            w_high(1, 0)
            w_high(1, 1)
            gate_copy(1, 0)
            w_high(1, 2)
            w_high(1, 3)
            gate_copy(1, 1)
            y_copy(0)
            gate_copy(1, 2)
            norm_apply(0)
            norm_T(0)
            gate_copy(1, 3)
            route_exp(1, 0.5)
            q_copy(0)
            k_copy(0)
            k_spread(0)
            route_T(1)
            v_copy(0)
            gate_copy(1, 4)
            soft_exp(0, 0)
            prob_T(0, 0)
            y_copy(1)
            soft_exp(0, 1)
            prob_T(0, 1)
            norm_apply(1)
            norm_T(1)
            soft_exp(0, 2)
            prob_T(0, 2)
            soft_exp(0, 3)
            q_copy(1)
            k_copy(1)
            prob_T(0, 3)
            k_spread(1)
            v_copy(1)
            att_T(0)
            soft_exp(1, 0)
            prob_T(1, 0)
            soft_exp(1, 1)
            prob_T(1, 1)
            norm_apply(2)
            norm_T(2)
            soft_exp(1, 2)
            soft_exp(1, 3)
            prob_T(1, 2)
            route_exp(2, 1.0)
            prob_T(1, 3)
            for i in range(FB):
                gelu(0, i)
                if i == 0:
                    route_T(2)
                    att_T(1)
                if i >= 1:
                    ffn_high(0, i - 1)
                if i == 6:
                    norm_apply(3)
                if i == 8:
                    norm_T(3)
                if i == 12:
                    route_exp(3, 1.0)
            route_T(3)
            ffn_high(0, FB - 1)
            gelu(1, 0)
            y_out(0)
            for i in range(1, FB):
                gelu(1, i)
                ffn_high(1, i - 1)
            ffn_high(1, FB - 1)
            y_out(1)

        @block.vector
        def _(dve):
            chain = [0]

            def link(ins):
                chain[0] += 1
                ins.then_inc(dve_chain, 1)
                dve.wait_ge(dve_chain, chain[0])

            def x_split(c):
                dve.wait_ge(act_x, c + 1)
                dve.tensor_tensor(xT_l[:, c], xT[:, c], xT_h[:, c].bitcast(F32), ALU.subtract).then_inc(dve_x, 1)

            def w_low(i):
                full, high, low, b = ((wgate, wgate_h, wgate_l, slice(SHARED, CB)), (wup, wup_h, wup_l, slice(SHARED, CB)),
                                      (wgate, wgate_h, wgate_l, slice(0, SHARED)), (wup, wup_h, wup_l, slice(0, SHARED)))[i]
                dve.wait_ge(act_wh, i + 1)
                dve.tensor_tensor(low[:, b], full[:, b], high[:, b].bitcast(F32), ALU.subtract).then_inc(dve_w, 1)

            def wide(v):
                return v.unsqueeze(2).broadcast_to([P, GROUPS, E])

            def route_max(j):
                if j >= 1:
                    dve.wait_ge(act_re, j)
                dve.wait_ge(pe_log, j + 1)
                L = b_rt[j][:, 0:GROUPS * E].rearrange("p (g e) -> p g e", e=E)
                if j < HALVES:
                    if j == 0:
                        dve.wait_ge(act_lg, 1)
                    link(dve.tensor_tensor(logit[:], L, logit_g[:].unsqueeze(1).broadcast_to([P, GROUPS, E]), ALU.add))
                    L = logit[:]
                for g in range(GROUPS):
                    ins = dve.max(top[:, g], L[:, g])
                link(ins)
                dve.tensor_tensor(rt[:, 0], L, wide(top[:, :, 0]), ALU.subtract).then_inc(dve_ld, 1)

            def route_pick(j):
                L = logit[:] if j < HALVES else b_rt[j][:, 0:GROUPS * E].rearrange("p (g e) -> p g e", e=E)
                for g in range(GROUPS):
                    ins = dve.max_index(topi[:, g], top[:, g], L[:, g])
                link(ins)
                ex = expert[:].unsqueeze(1).broadcast_to([P, GROUPS, E])
                for t in range(2):
                    ins = dve.tensor_tensor(rt[:, 1 + t], ex, wide(topi[:, :, t]), ALU.is_equal)
                link(ins)
                link(dve.tensor_tensor(rt[:, 3], rt[:, 1], rt[:, 2], ALU.add))

            def route(j):
                dve.wait_ge(act_re, j + 1)
                dve.tensor_tensor(rt[:, 4], expo[:], rt[:, 3], ALU.mult)
                link(dve.tensor_reduce(rs[:, 0], expo[:], AX_X, ALU.add))
                if j < HALVES:
                    link(dve.tensor_reduce(rs[:, 1], rt[:, 4], AX_X, ALU.add))
                    link(dve.scalar_tensor_tensor(rs[:, 2], rs[:, 0], 1e-20, rs[:, 1], ALU.mult, ALU.add))
                    link(dve.reciprocal(rs[:, 3], rs[:, 2]))
                else:
                    link(dve.reciprocal(rs[:, 3], rs[:, 0]))
                link(dve.tensor_tensor(rt[:, 4], rt[:, 4], wide(rs[:, 3]), ALU.mult))
                if j >= 1:
                    dve.wait_ge(pe_gT, j)
                link(dve.tensor_copy(wsplit[:, :, 0:E], rt[:, 4]))
                dve.tensor_tensor(wsplit[:, :, E:2 * E], rt[:, 4], wsplit[:, :, 0:E].bitcast(F32),
                                  ALU.subtract).then_inc(dve_split, 1)

            def gate_up(c, n):
                k = CB * c + n
                dve.wait_ge(act_g, k + 1)
                g = gate_s[:, k % 2]
                link(dve.scalar_tensor_tensor(leaky[:, k % 2], g, LEAK, g, ALU.mult, ALU.max))
                dve.wait_ge(pe_u, k + 1)
                if n == 2:
                    dve.wait_ge(pe_down, CB * c + 1)
                elif k > 2:
                    dve.wait_ge(dve_mid, k - 2 - (c and n > 2))
                dve.tensor_tensor(gu[:, k % 2], leaky[:, k % 2], b_h1[:], ALU.mult).then_inc(dve_gu, 1)

            def mids(c, n):
                k = ROUTED * c + n
                dve.wait_ge(dve_gu, CB * c + n + 2)
                dve.wait_ge(pe_wb, k + 1)
                if k >= 2:
                    dve.wait_ge(pe_down, CB * (c if n >= 2 else c - 1) + (n if n >= 2 else n + 4))
                dve.tensor_tensor(mid[:, n % 2], gu[:, (CB * c + n + 1) % 2], b_w[:], ALU.mult).then_inc(dve_mid, 1)

            def norm_stats(j):
                slot, c = j // HALVES, j % HALVES
                src = (y_tok, x1_tok)[slot][:, c]
                if slot == 0:
                    dve.wait_ge(act_y, c + 1)
                for g in range(GROUPS):
                    ins = dve.bn_stats(stat6[:, g], src[:, g])
                link(ins)
                if j:
                    dve.wait_ge(act_hn, j)
                for g in range(GROUPS):
                    ins = dve.bn_aggr(stat2[:, g], stat6[:, g])
                link(ins)

            def norm_rsqrt(j):
                norm_seed(j)
                norm_newton(j)

            def norm_seed(j):
                v, y, t, nb = (lnw[:, i] for i in range(4))
                link(dve.tensor_scalar(v, stat2[:, :, 1], EPS, None, ALU.add))
                link(dve.tensor_scalar(y.bitcast(I32), v.bitcast(I32), -0.5, float(RSQRT_SEED), ALU.mult, ALU.add))
                link(dve.tensor_tensor(t, y, y, ALU.mult))
                link(dve.tensor_tensor(t, t, v, ALU.mult))
                link(dve.scalar_tensor_tensor(nb, t, -10 / 3, t, ALU.add, ALU.mult))
                link(dve.scalar_tensor_tensor(y, nb, 5.0, y, ALU.add, ALU.mult))

            def norm_newton(j):
                v, y, t, nb = (lnw[:, i] for i in range(4))
                link(dve.tensor_tensor(t, y, y, ALU.mult))
                link(dve.scalar_tensor_tensor(t, t, -0.5 * HALLEY ** 3, v, ALU.mult, ALU.mult))
                link(dve.scalar_tensor_tensor(y, t, 1.5 * HALLEY, y, ALU.add, ALU.mult))
                dve.scalar_tensor_tensor(nb, stat2[:, :, 0], -1.0, y, ALU.mult, ALU.mult).then_inc(dve_rs, 1)

            def norm_apply(j):
                slot, c = j // HALVES, j % HALVES
                if c:
                    dve.wait_ge(pe_hT, j)
                for g in range(GROUPS // 2, GROUPS):
                    ins = dve.tensor_scalar(hn[:, slot, g], (y_tok, x1_tok)[slot][:, c, g], stat2[:, g, 0:1],
                                            lnw[:, 1, g:g + 1], ALU.subtract, ALU.mult)
                ins.then_inc(dve_hn, 1)

            def k_copy(c):
                dve.wait_ge(act_k, c + 1)
                if c:
                    dve.wait_ge(pe_s, RT * c)
                for h in range(HG // 2, HG):
                    ins = dve.tensor_scalar(kx[:, h], kT, headmask[:, h:h + 1], None, ALU.mult)
                ins.then_inc(dve_kx, 1)

            def norm_split(j):
                high, low = ((hT_h[:], hT_l[:]), (hT_h[:], hT_l[:]),
                             (h2_h[:, 0], h2_l[:, 0]), (h2_h[:, 1], h2_l[:, 1]))[j]
                dve.wait_ge(act_hT, j + 1)
                dve.tensor_tensor(low, hT[:, j // HALVES], high.bitcast(F32), ALU.subtract).then_inc(dve_hl, 1)

            def soft_max(c, r):
                dve.wait_ge(pe_s, RT * c + r + 1)
                s = b_s[c][r % 2][:].rearrange("p (q t) -> p q t", t=SEQ)
                link(dve.tensor_reduce(mx[:, r], s, AX_X, ALU.max))
                if c:
                    dve.wait_ge(pe_pT, RT * (c - 1) + r + 1)
                    if r < RT - 1:
                        dve.wait_ge(pool_sum, r + 1)
                dve.tensor_tensor(prob[:, r].rearrange("p (q t) -> p q t", t=SEQ), s,
                                  mx[:, r].unsqueeze(2).broadcast_to([P, GROUPS * HG, SEQ]),
                                  ALU.subtract).then_inc(dve_dif, 1)

            def last_sum(c):
                dve.wait_ge(act_exp, RT * (c + 1))
                dve.tensor_reduce(psum[:, :, RT - 1], prob[:, RT - 1].rearrange("p (g h t) -> p g h t", g=GROUPS, h=HG),
                                  AX_X, ALU.add).then_inc(dve_sum, 1)

            def attend(c):
                dve.wait_ge(pool_sum, (RT - 1) * (c + 1))
                dve.wait_ge(dve_sum, c + 1)
                link(dve.reciprocal(rsum[:], psum[:].rearrange("p g r h -> p (g r h)")))
                dve.wait_ge(pe_pv, RT * (c + 1))
                if c:
                    dve.wait_ge(pe_aT, c)
                dve.tensor_tensor(att.rearrange("p g (n d) -> p (g n) d", d=HD),
                                  b_ov[c][:].rearrange("p (q d) -> p q d", d=HD),
                                  rsum[:].unsqueeze(2).broadcast_to([P, GROUPS * HEADS, HD]),
                                  ALU.mult).then_inc(dve_att, 1)

            def residual(c):
                dve.wait_ge(pe_o, c + 1)
                dve.wait_ge(pool_yb, c + 1)
                dve.tensor_tensor(x1_tok[:, c], b_s[c][1][:].rearrange("p (g h) -> p g h", h=D), y_tok[:, c],
                                  ALU.add).then_inc(dve_x1, 1)
                dve.wait_ge(dve_x1, c + 1)

            def ffn(c, i):
                k = FB * c + i
                dve.wait_ge(act_gel, k + 1)
                if i % 2 == 0:
                    dve.wait_ge(pe_wb, ROUTED * HALVES + E * c + i // 2 + 1)
                if k == 0:
                    dve.wait_ge(pool_w1, FB // 4)
                if k >= SLOTS:
                    dve.wait_ge(act_ph, k - SLOTS + 1)
                    dve.wait_ge(*low_done(k - SLOTS))
                dve.tensor_tensor(pm[:, k % SLOTS], gel[k % SLOTS], b_we[c][i // 2 % len(b_we[c])][:],
                                  ALU.mult).then_inc(dve_pm, 1)

            def ffn_low(c, i):
                k = FB * c + i
                if not low_on_vector(c, i):
                    return
                dve.wait_ge(act_ph, k + 1)
                dve.wait_ge(dve_pm, k + 1)
                if k >= LAG:
                    dve.wait_ge(pe_y, k - LAG + 1)
                dve.tensor_tensor(p_l[:, k % LAG], pm[:, k % SLOTS], p_h[:, k % LAG].bitcast(F32),
                                  ALU.subtract).then_inc(dve_lo, 1)

            def finish(c):
                dve.wait_ge(pool_xo, c + 1)
                if c == 0:
                    dve.wait_ge(pe_yT, 1)
                    dve.tensor_tensor(o_tok[:, 0], b_o[:].rearrange("p (g h) -> p g h", h=D), x_tok[:, 0],
                                      ALU.add).then_inc(dve_out, 1)
                    return
                for g in range(GROUPS):
                    dve.wait_ge(pe_yT, g + 2)
                    dve.tensor_tensor(o_tok[:, 1, g], b_fin[g][:, 0:D], x_tok[:, 1, g], ALU.add).then_inc(dve_out, 1)

            for e in range(E):
                dve.memset(expert[:, e:e + 1], float(e)).then_inc(dve_const, 1)
            w_low(0)
            w_low(1)
            x_split(0)
            w_low(2)
            w_low(3)
            gate_up(0, 0)
            dve.wait_ge(pool_const, 3)
            for dst, src in ((sel_r, sel), (causal_r, causal[:])):
                dve.tensor_copy(dst[:], src).then_inc(dve_const, 1)
            dve.tensor_copy(ident_r[:], ident[0:SEQ, 0:SEQ].unsqueeze(1).broadcast_to([SEQ, GB, SEQ])
                            ).then_inc(dve_const, 1)
            dve.tensor_copy(selp_r[:].rearrange("k j (u m) -> k (j u) m", m=M), sel[:, :, 0:M]).then_inc(dve_const, 1)
            dve.tensor_reduce(headmask[:], head16[:].rearrange("p a h -> p h a"), AX_X, ALU.add).then_inc(dve_const, 1)
            dve.wait_ge(dve_const, E + 5)
            gate_up(0, 1)
            route_max(0)
            route_pick(0)
            route(0)
            x_split(1)
            gate_up(0, 2)
            mids(0, 0)
            gate_up(0, 3)
            mids(0, 1)
            gate_up(0, 4)
            dve.wait_ge(act_proj, 1)
            dve.tensor_copy(qkT_h[:], projT[:, 0:2]).then_inc(dve_qk, 1)
            mids(0, 2)
            gate_up(1, 0)
            dve.wait_ge(dve_qk, 1)
            dve.tensor_tensor(qkT_l[:], projT[:, 0:2], qkT_h[:].bitcast(F32), ALU.subtract).then_inc(dve_qk, 1)
            mids(0, 3)
            gate_up(1, 1)
            norm_stats(0)
            norm_rsqrt(0)
            norm_apply(0)
            gate_up(1, 2)
            route_max(1)
            norm_split(0)
            route_pick(1)
            route(1)
            k_copy(0)
            mids(1, 0)
            gate_up(1, 3)
            mids(1, 1)
            gate_up(1, 4)
            mids(1, 2)
            soft_max(0, 0)
            mids(1, 3)
            soft_max(0, 1)
            norm_stats(1)
            norm_rsqrt(1)
            norm_apply(1)
            soft_max(0, 2)
            soft_max(0, 3)
            norm_split(1)
            last_sum(0)
            k_copy(1)
            attend(0)
            soft_max(1, 0)
            soft_max(1, 1)
            residual(0)
            norm_stats(2)
            norm_rsqrt(2)
            norm_apply(2)
            soft_max(1, 2)
            soft_max(1, 3)
            norm_split(2)
            route_max(2)
            route_pick(2)
            last_sum(1)
            route(2)
            attend(1)
            for i in range(FB):
                ffn(0, i)
                if i >= 1:
                    ffn_low(0, i - 1)
                if i == 2:
                    residual(1)
                if i == 3:
                    norm_stats(3)
                if i == 4:
                    norm_seed(3)
                if i == 5:
                    norm_newton(3)
                if i == 6:
                    norm_apply(3)
                if i == 9:
                    norm_split(3)
                if i == 11:
                    route_max(3)
                    route_pick(3)
                if i == 13:
                    route(3)
            ffn_low(0, FB - 1)
            for i in range(FB):
                ffn(1, i)
                if i >= 1:
                    ffn_low(1, i - 1)
                if i == 4:
                    finish(0)
            ffn_low(1, FB - 1)
            finish(1)

        @block.tensor
        def _(pe):
            def three(dst, wh, wl, xh, xl, first, last, before_low=None):
                pe.matmul(dst, wh, xh, start=first, stop=False)
                pe.matmul(dst, wl, xh, start=False, stop=False)
                if before_low:
                    pe.wait_ge(*before_low)
                return pe.matmul(dst, wh, xl, start=False, stop=last)

            def keep_warm(bank, n):
                for _i in range(n):
                    pe.matmul(bank[:], wgate_h[:, SHARED],
                              wgate_h[:, SHARED].unsqueeze(1).broadcast_to([P, N // P, P]),
                              start=True, stop=True, skip_group_check=True)

            def x_T(c):
                pe.wait_ge(ld_x[c], 16 * GB)
                for g in range(GROUPS):
                    ins = pe.transpose(b_s[0][c][:, g * P:(g + 1) * P], x_tok[:, c, g], ident[:])
                ins.then_inc(pe_x, 1)

            def block_gate(c, n):
                k, j = CB * c + n, ORDER[n]
                if k < 2:
                    pe.wait_ge(dve_w, 2 * k + 2)
                if n == 0:
                    pe.wait_ge(act_xh, c + 1)
                if k >= 1:
                    pe.wait_ge(act_g, k)
                three(b_h0[:], wgate_h[:, j], wgate_l[:, j], xT_h[:, c], xT_l[:, c], True, True,
                      (dve_x, c + 1) if n == 0 else None).then_inc(pe_g, 1)

            def block_up(c, n):
                k, j = CB * c + n, ORDER[n]
                if k >= 1:
                    pe.wait_ge(dve_gu, k)
                three(b_h1[:], wup_h[:, j], wup_l[:, j], xT_h[:, c], xT_l[:, c], True, True).then_inc(pe_u, 1)

            def weights_up(c, n):
                j = ORDER[n + 1]
                if n == 0:
                    pe.wait_ge(act_gT, c + 1)
                if c or n:
                    pe.wait_ge(dve_mid, ROUTED * c + n)
                pe.matmul(b_w[:], selp_r[:, j], gT[:, 0], start=True, stop=True).then_inc(pe_wb, 1)

            def block_down(c, n):
                j = ORDER[n]
                if n == 0:
                    pe.wait_ge(dve_gu, CB * c + 1)
                    if c == 0:
                        pe.wait_ge(ld_down, 32)
                    else:
                        pe.wait_ge(act_y, c)
                else:
                    pe.wait_ge(dve_mid, ROUTED * c + n)
                src = gu[:, CB * c % 2] if n == 0 else mid[:, (n - 1) % 2]
                for g in range(GROUPS):
                    ins = pe.matmul(b_y[:, g * D:(g + 1) * D], src[:, g * P:(g + 1) * P], wdown[:, j],
                                    start=(n == 0 and g == 0), stop=(n == CB - 1), skip_group_check=True)
                ins.then_inc(pe_down, 1)

            def cond_logits(c):
                if c == 0:
                    pe.wait_ge(act_cols, 1)
                else:
                    pe.wait_ge(act_proj, 1)
                pe.wait_ge(act_x, c + 1)
                for g in range(GROUPS):
                    ins = pe.matmul(b_rt[c][:, g * E:(g + 1) * E], xT[:, c, g * P:(g + 1) * P],
                                    cols[:, ROW_WT:ROW_WT + E], start=True, stop=True)
                ins.then_inc(pe_log, 1)

            def condition_logits():
                pe.wait_ge(act_cols, 3)
                pe.matmul(b_t[:, 0:E], cond4[:].rearrange("k b s -> k (b s)"), gcols[:, GROW_WG:GROWS],
                          start=True, stop=True).then_inc(pe_lg, 1)

            def route_T(j):
                pe.wait_ge(dve_split, j + 1)
                for g in range(GROUPS):
                    ins = pe.transpose(b_rt[j][0:2 * E, g * P:(g + 1) * P], wsplit[:, g].bitcast(F32), ident[:])
                ins.then_inc(pe_gT, 1)

            def norm_T(j):
                pe.wait_ge(act_hn, j + 1)
                pe.wait_ge(dve_hn, j + 1)
                pe.wait_ge(*((act_lg, 1), (dve_mid, 2 * ROUTED), (act_pT, RT), (act_pT, 2 * RT))[j])
                for g in range(GROUPS):
                    ins = pe.transpose(b_tr[j % HALVES][:, g * P:(g + 1) * P], hn[:, j // HALVES, g], ident[:])
                ins.then_inc(pe_hT, 1)

            def qk(c):
                pe.wait_ge(dve_qk, 2)
                pe.wait_ge(act_hh, c + 1)
                pe.wait_ge(*((act_x, 2), (act_g, 2 * CB))[c])
                three(b_s[c][0][:], qkT_h[:, 0], qkT_l[:, 0], hT_h[:], hT_l[:], True, True,
                      (dve_hl, c + 1)).then_inc(pe_q, 1)
                if c:
                    pe.wait_ge(dve_gu, 2 * CB)
                three(b_s[c][1][:], qkT_h[:, 1], qkT_l[:, 1], hT_h[:], hT_l[:], True, True).then_inc(pe_k, 1)

            def values_up(c):
                pe.wait_ge(act_hT, c + 1)
                wv = projT[:, 2].rearrange("p (r h d) -> p h r d", r=RT, h=HG)
                for b in range(NB):
                    if c == 0 and b == NB // 2:
                        route_T(1)
                    for h in range(HG):
                        ins = pe.matmul(b_tr[c][h * SEQ:(h + 1) * SEQ, b * RT * HD:(b + 1) * RT * HD],
                                        hT[:, 0, b * SEQ:(b + 1) * SEQ], wv[:, h], start=True, stop=True)
                ins.then_inc(pe_v, 1)

            def scores(c, r):
                if r == 0:
                    pe.wait_ge(act_qk, c + 1)
                    pe.wait_ge(dve_kx, c + 1)
                elif r >= 2:
                    pe.wait_ge(dve_dif, RT * c + r - 1)
                dst = b_s[c][r % 2]
                pe.matmul(dst[:], ident_r[:].rearrange("k b s -> k (b s)"),
                          causal_r[:].unsqueeze(1).broadcast_to([SEQ, GROUPS * HG, SEQ]),
                          start=True, stop=False, skip_group_check=True)
                ch = slice(r * HG * HD, (r + 1) * HG * HD)
                for g in range(GROUPS):
                    for b in range(GB):
                        col = (g * GB + b) * SEQ
                        ins = pe.matmul(dst[b * SEQ:(b + 1) * SEQ, g * HG * SEQ:(g + 1) * HG * SEQ],
                                        qT[ch, col:col + SEQ], kx[ch, :, col:col + SEQ],
                                        start=False, stop=True, skip_group_check=True)
                ins.then_inc(pe_s, 1)

            def prob_T(c, r):
                pe.wait_ge(act_exp, RT * c + r + 1)
                if r == 0:
                    pe.wait_ge(act_v, c + 1)
                else:
                    pe.wait_ge(act_pT, RT * c + r)
                for g in range(GROUPS):
                    ins = pe.transpose(b_tr[c][:, g * P:(g + 1) * P], prob[:, r, g * P:(g + 1) * P], ident[:])
                ins.then_inc(pe_pT, 1)

            def values(c, r):
                pe.wait_ge(act_pT, RT * c + r + 1)
                pe.wait_ge(pool_vx, RT * c + r + 1)
                if r == 0:
                    pe.wait_ge(*((dve_split, 2), (act_y, 2))[c])
                    if c == 0:
                        pe.wait_ge(act_gT, 2)
                w = HG * HD
                for g in range(GROUPS):
                    for b in range(GB):
                        q = g * GB + b
                        ins = pe.matmul(b_ov[c][b * SEQ:(b + 1) * SEQ, g * D + r * w:g * D + (r + 1) * w],
                                        probT[:, r, q * SEQ:(q + 1) * SEQ], vx[:, q, r], start=True, stop=True)
                ins.then_inc(pe_pv, 1)

            def att_T(c):
                pe.wait_ge(dve_att, c + 1)
                for g in range(GROUPS):
                    ins = pe.transpose(b_s[c][0][:, g * P:(g + 1) * P], att[:, g], ident[:])
                ins.then_inc(pe_aT, 1)

            def project(c):
                pe.wait_ge(act_aT, c + 1)
                for g in range(GROUPS):
                    ins = pe.matmul(b_s[c][1][:, g * D:(g + 1) * D], attT[:, g * P:(g + 1) * P], projT[:, 3],
                                    start=True, stop=True)
                ins.then_inc(pe_o, 1)

            def ffn_logits(c):
                pe.wait_ge(act_hT, c + 3)
                for g in range(GROUPS):
                    ins = pe.matmul(b_rt[HALVES + c][:, g * E:(g + 1) * E], hT[:, 1, g * P:(g + 1) * P],
                                    cols[:, ROW_ROUTER:ROW_ROUTER + E], start=True, stop=True)
                ins.then_inc(pe_log, 1)

            def ffn_up(c, i):
                k = FB * c + i
                bank = b_h[c][i]
                if c == 0:
                    if i % 4 == 0:
                        pe.wait_ge(pool_w1, i // 4 + 1)
                if i == 0:
                    pe.wait_ge(act_hh, c + 3)
                earlier = [n for n, other in enumerate(b_h[0] + b_h[1]) if n < k and other is bank]
                if earlier:
                    pe.wait_ge(act_gel, earlier[-1] + 1)
                elif k < 2:
                    pe.wait_ge(*((act_aT, 1), (dve_x1, 1))[k])
                else:
                    pe.wait_ge(*((dve_x1, HALVES) if bank is b_h1 else (dve_pm, FB)))
                three(bank[:], w1_h[:, i], w1_l[:, i], h2_h[:, c], h2_l[:, c], True, True,
                      (dve_hl, c + 3) if i == 0 else None).then_inc(pe_h, 1)

            def ffn_weights(c, e):
                banks = b_we[c]
                if e == 0:
                    pe.wait_ge(act_gT, HALVES + c + 1)
                if (c, e) == (0, 1):
                    pe.wait_ge(act_aT, HALVES)
                elif (c, e) == (1, 1):
                    pe.wait_ge(dve_pm, FB - 2)
                elif e >= len(banks):
                    pe.wait_ge(dve_pm, FB * c + 2 * (e - len(banks)) + 2)
                pe.matmul(banks[e % len(banks)][:], sel_r[:, e], gT[:, GT_SLOT[HALVES + c]], start=True,
                          stop=True).then_inc(pe_wb, 1)

            def ffn_down(c, i):
                k = FB * c + i
                pe.wait_ge(act_ph, k + 1)
                if c == 0 and i % 4 == 0:
                    pe.wait_ge(pool_w2, i // 4 + 1)
                if i == 0:
                    pe.wait_ge(dve_att, c + 1)
                three(b_ov[c][:], w2_h[:, i], w2_l[:, i], p_h[:, k % LAG], p_l[:, k % LAG], i == 0, i == FB - 1,
                      low_done(k)).then_inc(pe_y, 1)

            def y_T(c):
                if c == 0:
                    pe.wait_ge(act_yT, 1)
                    for g in range(GROUPS):
                        ins = pe.transpose(b_o[:, g * P:(g + 1) * P], yT[:, g * P:(g + 1) * P], ident[:])
                    ins.then_inc(pe_yT, 1)
                    return
                pe.wait_ge(act_gel, HALVES * FB)
                for g in range(GROUPS):
                    pe.wait_ge(act_yT, g + 2)
                    pe.transpose(b_fin[g][:, 0:P], yT[:, g * P:(g + 1) * P], ident[:]).then_inc(pe_yT, 1)

            pe.wait_ge(pool_const, 1)
            x_T(0)
            pe.wait_ge(act_wh, 1)
            keep_warm(b_o, 2)
            block_gate(0, 0)
            block_up(0, 0)
            keep_warm(b_o, 1)
            block_gate(0, 1)
            block_up(0, 1)
            pe.wait_ge(ld_rows, 7 * 16)
            pe.wait_ge(ld_cond, 2 * 16)
            pe.wait_ge(pool_const, 2)
            pe.transpose(b_t[:, 0:ROWS], rows[:], ident[0:ROWS, 0:ROWS])
            pe.transpose(b_t[:, ROWS:ROWS + GROWS], grows[:], ident[0:GROWS, 0:GROWS]).then_inc(pe_cols, 1)
            condition_logits()
            cond_logits(0)
            block_down(0, 0)
            x_T(1)
            pe.wait_ge(ld_proj, 3 * 16)
            for k in range(4):
                ins = pe.transpose(b_o[:, k * P:(k + 1) * P], proj[:, k], ident[:])
            ins.then_inc(pe_proj, 1)
            block_gate(0, 2)
            block_up(0, 2)
            cond_logits(1)
            route_T(0)
            block_gate(0, 3)
            weights_up(0, 0)
            block_up(0, 3)
            block_down(0, 1)
            weights_up(0, 1)
            block_gate(0, 4)
            block_up(0, 4)
            block_down(0, 2)
            weights_up(0, 2)
            block_gate(1, 0)
            block_up(1, 0)
            block_down(0, 3)
            weights_up(0, 3)
            block_gate(1, 1)
            block_up(1, 1)
            block_down(0, 4)
            block_gate(1, 2)
            block_up(1, 2)
            block_gate(1, 3)
            block_down(1, 0)
            pe.wait_ge(act_x, 2)
            keep_warm(b_s0, 6)
            norm_T(0)
            block_up(1, 3)
            qk(0)
            values_up(0)
            weights_up(1, 0)
            scores(0, 0)
            block_down(1, 1)
            weights_up(1, 1)
            block_gate(1, 4)
            block_up(1, 4)
            weights_up(1, 2)
            scores(0, 1)
            block_down(1, 2)
            weights_up(1, 3)
            block_down(1, 3)
            prob_T(0, 0)
            block_down(1, 4)
            scores(0, 2)
            pe.wait_ge(act_y, 2)
            keep_warm(b_y, 3)
            values(0, 0)
            prob_T(0, 1)
            scores(0, 3)
            keep_warm(b_y, 2)
            values(0, 1)
            norm_T(1)
            keep_warm(b_y, 7)
            prob_T(0, 2)
            keep_warm(b_y, 4)
            values(0, 2)
            qk(1)
            prob_T(0, 3)
            values_up(1)
            values(0, 3)
            keep_warm(b_y, 3)
            att_T(0)
            scores(1, 0)
            keep_warm(b_y, 1)
            project(0)
            scores(1, 1)
            keep_warm(b_y, 1)
            prob_T(1, 0)
            scores(1, 2)
            keep_warm(b_y, 2)
            values(1, 0)
            prob_T(1, 1)
            scores(1, 3)
            values(1, 1)
            pe.wait_ge(act_aT, 1)
            keep_warm(b_s0, 2)
            norm_T(2)
            keep_warm(b_s0, 6)
            ffn_logits(0)
            prob_T(1, 2)
            ffn_up(0, 0)
            values(1, 2)
            prob_T(1, 3)
            ffn_up(0, 1)
            values(1, 3)
            route_T(2)
            att_T(1)
            ffn_weights(0, 0)
            for i in range(2, FB + LAG):
                if i == 3:
                    project(1)
                if i < FB:
                    ffn_up(0, i)
                    if i % 2 == 0:
                        ffn_weights(0, i // 2)
                if i >= LAG:
                    ffn_down(0, i - LAG)
                if i == 9:
                    norm_T(3)
                if i == 11:
                    ffn_logits(1)
                if i == 17:
                    route_T(3)
                if i == FB:
                    ffn_up(1, 0)
                if i == FB + 1:
                    ffn_up(1, 1)
            ffn_weights(1, 0)
            ffn_weights(1, 1)
            for i in range(2, FB + LAG):
                if i < FB:
                    ffn_up(1, i)
                    if i % 2 == 0 and i >= 4:
                        ffn_weights(1, i // 2)
                if i == 3:
                    y_T(0)
                if i >= LAG:
                    ffn_down(1, i - LAG)
            y_T(1)


_INS = ['x', 'cond_64', 'L0_cond_wt', 'L0_cond_wg', 'L0_cond_w_gate', 'L0_cond_w_up', 'L0_cond_w_down',
        'L0_cond_sw_gate', 'L0_cond_sw_up', 'L0_cond_sw_down', 'L0_ffn_ln1_w', 'L0_ffn_ln1_b',
        'L0_ffn_in_proj_w', 'L0_ffn_in_proj_b', 'L0_ffn_out_proj_w', 'L0_ffn_out_proj_b', 'L0_ffn_ln2_w',
        'L0_ffn_ln2_b', 'L0_ffn_router_w', 'L0_ffn_w1', 'L0_ffn_w2']


def kernel(**inputs):
    import numpy as _np
    import concourse.bacc as _bacc
    from concourse import mybir as _mybir
    from concourse.bass_utils import run_bass_kernel_spmd as _run

    nc = _bacc.Bacc("TRN2", target_bir_lowering=False, num_devices=1)
    arrays, args = {}, []
    for name in _INS:
        a = _np.ascontiguousarray(inputs[name])
        arrays[f"in_{name}"] = a
        args.append(nc.dram_tensor(f"in_{name}", a.shape, _mybir.dt.from_np(a.dtype), kind="ExternalInput").ap())
    shape = inputs['x'].shape
    args.append(nc.dram_tensor("out_0", shape, _mybir.dt.float32, kind="ExternalOutput").ap())
    build(nc, *args)
    r = _run(nc, [arrays], core_ids=[0])
    return r.results[0]["out_0"]
```
